# Optimizing a Trainium2 kernel written in Bass

```python
import numpy as np
import jax
import jax.numpy as jnp

def _softmax(x, axis=-1):
    return jax.nn.softmax(x, axis=axis)

def _gelu(x):
    return jax.nn.gelu(x, approximate=True)

def _silu(x):
    return jax.nn.silu(x)

def _sigmoid(x):
    return jax.nn.sigmoid(x)

def _layernorm(x, axis=-1, eps=1e-05):
    m = jnp.mean(x, axis=axis, keepdims=True)
    v = jnp.var(x, axis=axis, keepdims=True)
    return (x - m) / jnp.sqrt(v + eps)

def _scatter_add(tgt, idx, src, axis=0):
    return tgt.at[idx].add(src)

def _segment_sum(src, seg, n):
    return jax.ops.segment_sum(src, seg, n)
kernel_name = 'mk_seq_postln_d1_jaxref_r8_642313'

def setup_inputs(seed: int=0):
    np.random.seed(seed)
    _w = jnp.asarray

    def _L0_attn_setup():
        import jax, jax.numpy as jnp
        import numpy as np
        D_MODEL = 128
        NUM_HEADS = 16
        HEAD_DIM = D_MODEL // NUM_HEADS
        ALPHA = 1.0
        key = jax.random.key(seed)
        ks = jax.random.split(key, 9)
        B, T, D = (2, 256, D_MODEL)
        s = 1.0 / np.sqrt(D)
        inp = {'x': jax.random.normal(ks[0], (B, T, D), dtype=jnp.float32), 'Wq': jax.random.uniform(ks[1], (D, D), jnp.float32, -s, s), 'bq': jax.random.uniform(ks[2], (D,), jnp.float32, -s, s), 'Wk': jax.random.uniform(ks[3], (D, D), jnp.float32, -s, s), 'bk': jax.random.uniform(ks[4], (D,), jnp.float32, -s, s), 'Wv': jax.random.uniform(ks[5], (D, D), jnp.float32, -s, s), 'bv': jax.random.uniform(ks[6], (D,), jnp.float32, -s, s), 'Wo': jax.random.uniform(ks[7], (D, D), jnp.float32, -s, s), 'bo': jax.random.uniform(ks[8], (D,), jnp.float32, -s, s)}
        return inp
    _L0_attn_in = _L0_attn_setup()

    def _L0_ffn_setup():
        import jax, jax.numpy as jnp
        import numpy as np
        D_IN, D_HID = (128, 512)

        def _ternary(key, shape):
            return jax.random.randint(key, shape, -1, 2).astype(jnp.float32)

        def _tlin(x, w, s):
            return jnp.einsum('bsi,oi->bso', x, w) * s
        key = jax.random.key(seed)
        ks = jax.random.split(key, 12)
        inv = lambda fan: 1.0 / np.sqrt(fan).astype(np.float32)
        return {'x': jax.random.normal(ks[0], (4, 256, D_IN), dtype=jnp.float32), 'w1_w': _ternary(ks[1], (D_HID, D_IN)), 'w1_s': jax.random.uniform(ks[2], (D_HID,), dtype=jnp.float32) * inv(D_IN), 'w2_w': _ternary(ks[3], (D_HID, D_IN)), 'w2_s': jax.random.uniform(ks[4], (D_HID,), dtype=jnp.float32) * inv(D_IN), 'h1_w': _ternary(ks[5], (D_HID, D_HID)), 'h1_s': jax.random.uniform(ks[6], (D_HID,), dtype=jnp.float32) * inv(D_HID), 'h2_w': _ternary(ks[7], (D_HID, D_HID)), 'h2_s': jax.random.uniform(ks[8], (D_HID,), dtype=jnp.float32) * inv(D_HID), 'w3_w': _ternary(ks[9], (D_IN, D_HID)), 'w3_s': jax.random.uniform(ks[10], (D_IN,), dtype=jnp.float32) * inv(D_HID)}
    _L0_ffn_in = _L0_ffn_setup()
    _d = {'L0_attn_x': _L0_attn_in['x'], 'L0_attn_Wq': _L0_attn_in['Wq'], 'L0_attn_bq': _L0_attn_in['bq'], 'L0_attn_Wk': _L0_attn_in['Wk'], 'L0_attn_bk': _L0_attn_in['bk'], 'L0_attn_Wv': _L0_attn_in['Wv'], 'L0_attn_bv': _L0_attn_in['bv'], 'L0_attn_Wo': _L0_attn_in['Wo'], 'L0_attn_bo': _L0_attn_in['bo'], 'L0_ffn_w1_w': _L0_ffn_in['w1_w'], 'L0_ffn_w1_s': _L0_ffn_in['w1_s'], 'L0_ffn_w2_w': _L0_ffn_in['w2_w'], 'L0_ffn_w2_s': _L0_ffn_in['w2_s'], 'L0_ffn_h1_w': _L0_ffn_in['h1_w'], 'L0_ffn_h1_s': _L0_ffn_in['h1_s'], 'L0_ffn_h2_w': _L0_ffn_in['h2_w'], 'L0_ffn_h2_s': _L0_ffn_in['h2_s'], 'L0_ffn_w3_w': _L0_ffn_in['w3_w'], 'L0_ffn_w3_s': _L0_ffn_in['w3_s']}
    _x0 = _d['L0_attn_x']
    _d['L0_attn_x'] = jax.random.normal(jax.random.fold_in(jax.random.key(seed), 1), (32, 256, 128), dtype=_x0.dtype)
    del _x0
    return _d

def reference(L0_attn_x, L0_attn_Wq, L0_attn_bq, L0_attn_Wk, L0_attn_bk, L0_attn_Wv, L0_attn_bv, L0_attn_Wo, L0_attn_bo, L0_ffn_w1_w, L0_ffn_w1_s, L0_ffn_w2_w, L0_ffn_w2_s, L0_ffn_h1_w, L0_ffn_h1_s, L0_ffn_h2_w, L0_ffn_h2_s, L0_ffn_w3_w, L0_ffn_w3_s):

    def _L0_attn_ref(x, Wq, bq, Wk, bk, Wv, bv, Wo, bo):
        import jax, jax.numpy as jnp
        import numpy as np
        D_MODEL = 128
        NUM_HEADS = 16
        HEAD_DIM = D_MODEL // NUM_HEADS
        ALPHA = 1.0
        B, T, D = x.shape
        H, hd = (NUM_HEADS, HEAD_DIM)

        def split_heads(y):
            return y.reshape(B, T, H, hd).transpose(0, 2, 1, 3)
        Q = split_heads(x @ Wq.T + bq)
        K = split_heads(x @ Wk.T + bk)
        V = split_heads(x @ Wv.T + bv)
        scores = jnp.einsum('bhid,bhjd->bhij', Q, K) / jnp.sqrt(jnp.float32(hd))
        t = jnp.arange(T)
        delta = t[:, None] - t[None, :]
        causal_mask = delta < 0
        decay = jnp.where(causal_mask, 0.0, -delta.astype(jnp.float32) ** ALPHA)
        scores = jnp.where(causal_mask, -jnp.inf, scores) + decay
        attn = jax.nn.softmax(scores, axis=-1)
        out = jnp.einsum('bhij,bhjd->bhid', attn, V)
        out = out.transpose(0, 2, 1, 3).reshape(B, T, D)
        return out @ Wo.T + bo

    def _L0_ffn_ref(x, w1_w, w1_s, w2_w, w2_s, h1_w, h1_s, h2_w, h2_s, w3_w, w3_s):
        import jax, jax.numpy as jnp
        import numpy as np
        D_IN, D_HID = (128, 512)

        def _ternary(key, shape):
            return jax.random.randint(key, shape, -1, 2).astype(jnp.float32)

        def _tlin(x, w, s):
            return jnp.einsum('bsi,oi->bso', x, w) * s
        h = jax.nn.silu(_tlin(x, w1_w, w1_s)) * _tlin(x, w2_w, w2_s)
        h = jax.nn.gelu(_tlin(h, h1_w, h1_s), approximate=False)
        h = jax.nn.gelu(_tlin(h, h2_w, h2_s), approximate=False)
        return _tlin(h, w3_w, w3_s)
    x = L0_attn_x
    x = _layernorm(x + _L0_attn_ref(x, L0_attn_Wq, L0_attn_bq, L0_attn_Wk, L0_attn_bk, L0_attn_Wv, L0_attn_bv, L0_attn_Wo, L0_attn_bo), axis=-1)
    x = _layernorm(x + _L0_ffn_ref(x, L0_ffn_w1_w, L0_ffn_w1_s, L0_ffn_w2_w, L0_ffn_w2_s, L0_ffn_h1_w, L0_ffn_h1_s, L0_ffn_h2_w, L0_ffn_h2_s, L0_ffn_w3_w, L0_ffn_w3_s), axis=-1)
    return x

_drawn_inputs = setup_inputs


def setup_inputs(seed=0):
    import zlib

    import numpy as np

    out = dict(_drawn_inputs(seed))
    spreads = {}
    factors = {'L0_attn_bq': 8.0,
     'L0_attn_bk': 8.0,
     'L0_ffn_w1_w': 8.0,
     'L0_ffn_w1_s': 8.0,
     'L0_ffn_w2_w': 8.0,
     'L0_ffn_w2_s': 8.0,
     'L0_ffn_h1_w': 8.0,
     'L0_ffn_h1_s': 8.0,
     'L0_ffn_h2_w': 8.0,
     'L0_ffn_h2_s': 8.0,
     'L0_ffn_w3_w': 8.0,
     'L0_ffn_w3_s': 8.0}
    for name, (base, spread) in spreads.items():
        noise = np.random.default_rng([zlib.crc32(name.encode()), seed]).standard_normal(out[name].shape)
        drawn = base * np.exp(spread * noise) if base else spread * noise
        out[name] = jnp.asarray(drawn.astype(out[name].dtype))
    for name, factor in factors.items():
        out[name] = (out[name] * factor).astype(out[name].dtype)
    return out
```

```python
from contextlib import ExitStack

import numpy as np

import concourse.bass as bass
from concourse import mybir

F32 = mybir.dt.float32
F32R = mybir.dt.float32r
BF16 = mybir.dt.bfloat16
I32 = mybir.dt.int32
ALU = mybir.AluOpType
ACT = mybir.ActivationFunctionType
AX_X = mybir.AxisListType.X

P = 128
B, T, D = 32, 256, 128
H, HD = 16, 8
FF = 512
KT = FF // P
PAIRS = B // 2
TOK = 2 * T
TT = TOK // P
U, C = 4, 4
BIG = -(2.0 ** 100)
EPS = 1e-5

ROW_DATA, ROW_MAX, ROWS = 4, 28, 30
Q_PARTS, K_PARTS = "hlh", "hhl"

AFTER_S = {
    0: [("pv", 1, 3), ("gu", 0)], 1: [("araw", 1), ("gu", 1)], 2: [("atr", 1), ("gu", 2)],
    3: [("anorm", 1), ("gu", 3)], 4: [("atT", 1)], 5: [("wo",), ("h", 1, 0)],
    6: [("zt", 1), ("lnstat", 1), ("h", 1, 1)], 7: [("h", 1, 2)], 8: [("lnnorm", 1), ("h", 1, 3)],
    9: [("qx",)], 10: [("mT", 0), ("h", 2, 0)], 11: [("qq",), ("h", 2, 1)], 12: [("h", 2, 2)],
    13: [("qk",), ("h", 2, 3)], 15: [("qv",)],
}
AFTER_ST = {
    0: [("w3",)], 2: [("mT", 1)], 3: [("zt", 2), ("lnstat", 2)], 4: [("xload",)],
    6: [("lnnorm", 2)], 7: [("x1t",)], 10: [("araw", 0)], 11: [("atr", 0)], 13: [("anorm", 0)],
    14: [("atT", 0)],
}
HP = H // 2


def make_schedule():
    steps = []
    for n in range(2 * HP):
        steps.append(("s", n // HP, n % HP))
        if n % HP == HP - 1:
            steps.append(("max", n // HP))
        steps += AFTER_S.get(n, [])
    for n in range(2 * HP):
        steps.append(("st", n // HP, n % HP))
        if n % 2 == 1:
            g = n // 2
            steps.append(("sel", g // U, g % U))
            if g:
                steps.append(("pv", (g - 1) // U, (g - 1) % U))
        steps += AFTER_ST.get(n, [])
    return steps


def scores_first(schedule, kind, keep=()):
    order, held = [], []
    last = max(i for i, s in enumerate(schedule) if s[0] == kind)
    first = min(i for i, s in enumerate(schedule) if s[0] == kind)
    for i, s in enumerate(schedule):
        if s[0] == kind:
            order.append(s)
            order += held
            held = []
        elif first < i < last and s[0] not in keep:
            held.append(s)
        else:
            order.append(s)
    return order + held


SCHEDULE = make_schedule()
DVE_SCHEDULE = scores_first(SCHEDULE, "s", keep=("max",))
ACT_SCHEDULE = scores_first(SCHEDULE, "st")
STAGE_L = [("pv", 1, 3), ("araw", 1), ("atr", 1), ("anorm", 1), ("atT", 1),
           ("wo",), ("zt", 1), ("lnstat", 1), ("lnnorm", 1), ("x1t",)]
PAIR_OF_STAGE = {"Q": 1, "A": 0, "L": -1, "F": -2, "X": 2}


def stage_of(s):
    if s in STAGE_L:
        return "L"
    if s[0] in ("qx", "qq", "qk", "qv"):
        return "Q"
    if s[0] in ("gu", "h", "w3", "zt", "lnstat", "lnnorm"):
        return "F"
    return "X" if s[0] == "xload" else "A"


F_UNITS = [(n, m) for m in range(KT) for n in ("g", "u")] + [("h", i, m) for i in (1, 2) for m in range(KT)]
F_BY_ACT = [u for u in F_UNITS if u[0] != "u"]
ONE_KINDS = ("qx", "qq", "qk", "qv", "mT", "atr", "atT", "wo", "zt", "x1t", "w3")
ONE_UNITS = [s for s in SCHEDULE if s[0] in ONE_KINDS]


def build_layer(nc, x, wq, wk, wv, wo, vecs, bv, w1, w2, h1, h2, w3, qrows, krows, out):
    ctx = ExitStack()
    with ctx:
        def sb(name, shape, dt=F32):
            return ctx.enter_context(nc.sbuf_tensor(name, shape, dt))

        def sem(name):
            return ctx.enter_context(nc.semaphore(name))

        class Signal:

            def __init__(self, name, per, unit=1):
                self.sem, self.per, self.unit = sem(name), per, unit

            def wait(self, eng, pair, k=None):
                v = (pair * self.per + (self.per if k is None else k)) * self.unit
                if isinstance(v, int) and v <= 0:
                    return
                eng.wait_ge(self.sem, v)

        wq_sb, wk_sb = sb("wq_sb", [P, D]), sb("wk_sb", [P, D])
        wv_sb, wo_sb = sb("wv_sb", [P, D]), sb("wo_sb", [P, D])
        vec_sb = sb("vec_sb", [P, 4 + 4 * KT])
        bq_scaled = sb("bq_scaled", [P, 1])
        bv_sb = sb("bv_sb", [P, D])
        ident = sb("ident", [P, P])
        ident_bf = sb("ident_bf", [P, P], BF16)
        mask2 = sb("mask2", [P, 2, P], BF16)
        neg_half = sb("neg_half", [P, TT])
        ones_col = sb("ones_col", [P, 1])
        SPLIT = (("w1", FF), ("w2", FF), ("h1", KT * FF), ("h2", KT * FF), ("w3", KT * D))
        w_hi = {n: sb(n + "_hi", [P, c], F32R) for n, c in SPLIT}
        w_lo = {n: sb(n + "_lo", [P, c], F32R) for n, c in SPLIT}
        lo_max = sb("lo_max", [P, len(SPLIT)])
        lo_all = sb("lo_all", [P, 1])
        lo_flag = sb("lo_flag", [1, 1])

        x_tok = sb("x_tok", [P, TT, D])
        xT = [sb(f"xT{i}", [P, TOK]) for i in range(2)]
        qk32 = [sb("q32", [P, TOK]), sb("k32", [P, TOK])]
        qk_hi = [sb("q_hi", [P, TOK], F32R), sb("k_hi", [P, TOK], F32R)]
        qk_lo = [sb("q_lo", [P, TOK], F32R), sb("k_lo", [P, TOK], F32R)]
        qs = [sb(f"qs{i}", [P, U, TOK], F32R) for i in range(2)]
        ks = [sb(f"ks{i}", [P, U, TOK], F32R) for i in range(2)]
        vst = [sb(f"vst{i}", [P, TT, U, C, 32]) for i in range(2)]

        mx3 = sb("mx3", [P, C, U, 3])
        m32 = sb("m32", [P, 2, C, U])
        mhl = sb("mhl", [P, 2, C, 2, U])
        mT_sb = sb("mT_sb", [32, T], F32R)
        pt = [sb(f"pt{i}", [P, C, 3 * P]) for i in range(2)]
        raw = sb("raw", [P, TOK])
        rT = sb("rT", [P, 4, P])
        rec = sb("rec", [P, 4, C, 2])
        attn = sb("attn", [P, 2, D])
        attT = sb("attT", [P, TOK])

        zT = [sb(f"zT{i}", [P, TOK]) for i in (1, 2)]
        st6 = [sb(f"st6_{i}", [P, TT, 6]) for i in (1, 2)]
        mv = [sb(f"mv{i}", [P, TT, 2]) for i in (1, 2)]
        ve = [sb(f"ve{i}", [P, TT]) for i in (1, 2)]
        rstd = [sb(f"rstd{i}", [P, TT]) for i in (1, 2)]
        x1 = sb("x1", [P, TT, D])
        x1T = sb("x1T", [P, TOK])
        x1hi, x1lo = sb("x1hi", [P, TOK], F32R), sb("x1lo", [P, TOK], F32R)
        sg = sb("sg", [P, 2, TOK])
        hf = sb("hf", [P, 4, TOK])
        h_hi = [sb(f"hhi{i}", [P, KT, TOK], F32R) for i in range(2)]
        h_lo = [sb(f"hlo{i}", [P, KT, TOK], F32R) for i in range(2)]
        o_tok = sb("o_tok", [P, TT, D])

        ps = ctx.enter_context(nc.psum_tensor("ps", [P, 8, TOK], F32))
        SCORE, FB, PVB, ONE = ((0, 1), (2, 3)), (4, 5), 6, 7

        w_in = sem("w_in")
        hw_in = [sem(f"hw_in{i}") for i in range(2)]
        pool_const = sem("pool_const")
        split_hi, split_lo, split_mx = sem("split_hi"), sem("split_lo"), sem("split_mx")
        lo_summed, flag_ready, consts_ready = sem("lo_summed"), sem("flag_ready"), sem("consts_ready")
        x_loaded = Signal("x_loaded", 1, 16)
        q_full = Signal("q_full", 4)
        xT_ready = Signal("xT_ready", 1)
        qk32_ready = Signal("qk32_ready", 2)
        qkhi_ready = Signal("qkhi_ready", 2)
        qklo_ready = Signal("qklo_ready", 2)
        v_ready = Signal("v_ready", 2)
        stacked = Signal("stacked", 24, 16)
        s_full = Signal("s_full", 2 * HP)
        s_free = Signal("s_free", 2 * HP)
        m_step = Signal("m_step", 8)
        mT_full = Signal("mT_full", 2)
        mT_ready = Signal("mT_ready", 2)
        m_sent = Signal("m_sent", 8, 16)
        t_full = Signal("t_full", 2 * HP)
        t_free = Signal("t_free", 2 * HP)
        masked = Signal("masked", 8)
        pv_done = Signal("pv_done", 8)
        raw_ready = Signal("raw_ready", 2)
        at_full = Signal("at_full", 4)
        rT_ready = Signal("rT_ready", 2)
        rec_ready = Signal("rec_ready", 2)
        attn_ready = Signal("attn_ready", 8)
        attT_ready = Signal("attT_ready", 2)
        l_full = Signal("l_full", 3)
        e_full = Signal("e_full", 2)
        f_full = Signal("f_full", len(F_UNITS))
        f_act = Signal("f_act", len(F_BY_ACT))
        f_dve = Signal("f_dve", KT)
        zT_ready = [Signal(f"zT{i}_ready", 1) for i in (1, 2)]
        ln_stats = [Signal(f"ln{i}_stats", TT) for i in (1, 2)]
        ln_mv = [Signal(f"ln{i}_mv", TT) for i in (1, 2)]
        ln_ve = [Signal(f"ln{i}_ve", 1) for i in (1, 2)]
        ln_rstd = [Signal(f"ln{i}_rstd", 1) for i in (1, 2)]
        ln_part = [Signal(f"ln{i}_part", TT) for i in (1, 2)]
        x1T_ready = Signal("x1T_ready", 1)
        x1hi_ready = Signal("x1hi_ready", 1)
        x1lo_ready = Signal("x1lo_ready", 1)
        h0hi_ready = Signal("h0hi_ready", KT)
        hhi_ready = Signal("hhi_ready", 2 * KT)
        hlo_ready = Signal("hlo_ready", 3 * KT)
        stored = Signal("stored", 1, 16)

        one_read = {("qx",): (xT_ready, 1), ("qq",): (qk32_ready, 1), ("qk",): (qk32_ready, 2),
                    ("qv",): (v_ready, 2), ("mT", 0): (mT_ready, 1), ("mT", 1): (mT_ready, 2),
                    ("atr", 0): (rT_ready, 1), ("atr", 1): (rT_ready, 2),
                    ("atT", 0): (attT_ready, 1), ("atT", 1): (attT_ready, 2),
                    ("wo",): (zT_ready[0], 1), ("w3",): (zT_ready[1], 1), ("x1t",): (x1T_ready, 1),
                    ("zt", 1): (ln_part[0], TT), ("zt", 2): (ln_part[1], TT)}

        def wait_one(eng, s, t, stages, before):
            uses = [(v, t - 1) for v in ONE_UNITS if stage_of(v) in before]
            uses += [(v, t) for v in ONE_UNITS[:ONE_UNITS.index(s)] if stage_of(v) in stages]
            if uses:
                v, of = uses[-1]
                signal, k = one_read[v]
                signal.wait(eng, of + PAIR_OF_STAGE[stage_of(v)], k)

        def wait_score_banks(eng, n, pair):
            if n < 2:
                t_free.wait(eng, pair - 1, n - 2 + 2 * HP + 1)
            elif n < 2 * HP + 2:
                s_free.wait(eng, pair, n - 1)
            else:
                t_free.wait(eng, pair, n - 2 * HP - 1)

        def wait_f_bank(eng, unit, pair):
            n = F_UNITS.index(unit)
            if n < 2:
                pair = pair - 1
            last = F_UNITS[n - 2]
            if last in F_BY_ACT:
                f_act.wait(eng, pair, F_BY_ACT.index(last) + 1)
            else:
                f_dve.wait(eng, pair, last[1] + 1)

        def slots(eng, slot):
            full = "ALQFX"
            slot(-1, 1, "QX", "")
            slot(0, 0, "AQX", "QX")
            slot(1, 1, "ALQX", "AQX")
            slot(2, 0, full, "ALQX")
            slot(3, 1, full, full)
            with eng.Fori(0, (PAIRS - 6) // 2) as i:
                slot(2 * i + 4, 0, full, full)
                slot(2 * i + 5, 1, full, full)
            slot(PAIRS - 2, 0, "ALQF", full)
            slot(PAIRS - 1, 1, "ALF", "ALQF")
            slot(PAIRS, 0, "LF", "ALF")
            slot(PAIRS + 1, 1, "F", "LF")

        def steps(t, par, stages, schedule=SCHEDULE):
            for s in schedule:
                stage = stage_of(s)
                if stage in stages:
                    d = PAIR_OF_STAGE[stage]
                    yield s, t + d, (par + d) % 2

        steps_passed = {n: sem("passed_" + n) for n in ("sp", "dve", "pool")}

        def carry(eng, name):
            eng.sem_inc(steps_passed[name], 1)

        block = ctx.enter_context(nc.Block())

        @block.sync
        def _(sp):
            for dst, src in ((wq_sb, wq), (wk_sb, wk), (wv_sb, wv), (wo_sb, wo), (vec_sb, vecs)):
                sp.dma_start(dst[:], src).then_inc(w_in, 16)
            sp.dma_start(bv_sb[:], bv.broadcast_to([P, D])).then_inc(w_in, 16)
            sp.dma_start(hf[:, 0, :], w1).then_inc(w_in, 16)
            sp.dma_start(hf[:, 1, :], w2).then_inc(w_in, 16)
            sp.dma_start(hf[:, 2, :], w3).then_inc(w_in, 16)
            sp.dma_start(qk32[0][:], qrows).then_inc(w_in, 16)
            sp.dma_start(qk32[1][:], krows).then_inc(w_in, 16)
            for i, src in enumerate((h1, h2)):
                sp.dma_start(vst[i][:].rearrange("p a b c d -> p (a b c d)"), src).then_inc(hw_in[i], 16)

            def load_x(q):
                sp.dma_start(x_tok[:], x[q]).then_inc(x_loaded.sem, 16)

            load_x(0)
            sp.wait_ge(consts_ready, 1)

            def slot(t, par, stages, before):
                for s, q, p in steps(t, par, stages):
                    kind = s[0]
                    if kind == "xload":
                        q_full.wait(sp, q - 1, 1)
                        carry(sp, "sp")
                        load_x(q)
                    elif kind in ("qq", "qk"):
                        w = ("qq", "qk").index(kind)
                        stack = (qs, ks)[w][p]
                        t_full.wait(sp, q - 2)
                        carry(sp, "sp")
                        qklo_ready.wait(sp, q, w + 1)
                        carry(sp, "sp")
                        for part, letter in enumerate((Q_PARTS, K_PARTS)[w]):
                            src = (qk_hi if letter == "h" else qk_lo)[w]
                            for c in range(C):
                                r = 32 * c + ROW_DATA + HD * part
                                sp.dma_start(stack[r:r + HD, :, :].bitcast(F32),
                                             src[32 * c:32 * c + 32, :].bitcast(F32)
                                             ).then_inc(stacked.sem, 16)
                    elif kind == "mT":
                        b = s[1]
                        mT_ready.wait(sp, q, b + 1)
                        carry(sp, "sp")
                        for c in range(C):
                            r = 32 * c + ROW_MAX
                            sp.dma_start(qs[p][r:r + 2, :, b * T:(b + 1) * T].bitcast(F32),
                                         mT_sb[8 * c:8 * c + 8, :].bitcast(F32)).then_inc(m_sent.sem, 16)
                    elif kind == "lnnorm" and s[1] == 2:
                        ln_part[1].wait(sp, q)
                        carry(sp, "sp")
                        sp.dma_start(out[q], o_tok[:]).then_inc(stored.sem, 16)

            slots(sp, slot)
            stored.wait(sp, PAIRS - 1)

        @block.tensor
        def _(pe):
            def program(split_weights):
                def ff_group(acc, name, col, hi, lo, wait_hi, wait_lo):
                    n = len(col)
                    for k in range(n):
                        wait_hi(k)
                        pe.matmul(acc, w_hi[name][:, col[k]:col[k] + P], hi(k), start=(k == 0), stop=False)
                        if split_weights:
                            pe.matmul(acc, w_lo[name][:, col[k]:col[k] + P], hi(k),
                                      start=False, stop=False)
                    for k in range(n):
                        wait_lo(k)
                        last = pe.matmul(acc, w_hi[name][:, col[k]:col[k] + P], lo(k),
                                         start=False, stop=(k == n - 1))
                    return last

                def slot(t, par, stages, before):
                    for s, q, p in steps(t, par, stages):
                        kind = s[0]
                        if kind in ONE_KINDS:
                            wait_one(pe, s, t, stages, before)
                        if kind == "qx":
                            x_loaded.wait(pe, q)
                            for j in range(TT):
                                last = pe.transpose(ps[:, ONE, j * P:(j + 1) * P], x_tok[:, j, :], ident[:])
                            last.then_inc(q_full.sem, 1)
                        elif kind in ("qq", "qk"):
                            w = ("qq", "qk").index(kind)
                            xT_ready.wait(pe, q)
                            pe.matmul(ps[:, ONE, :], (wq_sb, wk_sb)[w][:], xT[p][:],
                                      start=True, stop=True).then_inc(q_full.sem, 1)
                        elif kind == "qv":
                            for j in range(TT):
                                last = pe.matmul(ps[:, ONE, j * P:(j + 1) * P], xT[p][:, j * P:(j + 1) * P],
                                                 wv_sb[:], start=True, stop=True)
                            last.then_inc(q_full.sem, 1)
                        elif kind == "s":
                            _, b, n = s
                            u, banks = n // 2, SCORE[n % 2]
                            if (b, n) == (0, 0):
                                stacked.wait(pe, q)
                            wait_score_banks(pe, HP * b + n, q)
                            for e, bank in enumerate(banks):
                                c = 2 * (n % 2) + e
                                qr = qs[p][32 * c:32 * c + ROW_MAX, u, b * T:(b + 1) * T]
                                kr = ks[p][32 * c:32 * c + ROW_MAX, u, b * T:(b + 1) * T]
                                pe.matmul(ps[:, bank, 0:T], qr[:, P:T], kr, start=True, stop=False,
                                          skip_group_check=True)
                                pe.matmul(ps[:, bank, T:T + P], qr[:, 0:P], kr[:, 0:P], start=False,
                                          stop=False, skip_group_check=True)
                                last = pe.matmul(ps[:, bank, P:T + P], ident_bf[:],
                                                 mask2[:].rearrange("p a k -> p (a k)"),
                                                 start=False, stop=True, skip_group_check=True)
                            last.then_inc(s_full.sem, 1)
                        elif kind == "mT":
                            b = s[1]
                            m_step.wait(pe, q, 4 * b + 4)
                            for it in range(2):
                                last = pe.transpose(ps[0:32, ONE, it * P:(it + 1) * P],
                                                    mhl[:, it].rearrange("p c a u -> p (c a u)"), ident[:])
                            last.then_inc(mT_full.sem, 1)
                        elif kind == "st":
                            _, b, n = s
                            u, banks = n // 2, SCORE[n % 2]
                            if n == 0:
                                m_sent.wait(pe, q, 4 * b + 4)
                            wait_score_banks(pe, 2 * HP + HP * b + n, q)
                            for e, bank in enumerate(banks):
                                c = 2 * (n % 2) + e
                                qr = qs[p][32 * c:32 * c + ROWS, u, b * T:(b + 1) * T]
                                kr = ks[p][32 * c:32 * c + ROWS, u, b * T:(b + 1) * T]
                                pe.matmul(ps[:, bank, 0:P], kr[:, P:T], qr[:, P:T], start=True, stop=False,
                                          skip_group_check=True)
                                last = pe.matmul(ps[:, bank, P:P + T], kr[:, 0:P], qr, start=False,
                                                 stop=True, skip_group_check=True)
                            last.then_inc(t_full.sem, 1)
                        elif kind == "pv":
                            _, b, u = s
                            half, odd = u // 2, u % 2
                            masked.wait(pe, q, 4 * b + u + 1)
                            if u == 0:
                                if b == 0:
                                    v_ready.wait(pe, q)
                                raw_ready.wait(pe, q, b)
                            o = half * T
                            for kb in (0, 1):
                                for c in range(C):
                                    acc = ps[32 * c:32 * c + 32, PVB, o + P * kb:o + T]
                                    pr = pt[u % 2][:, c, P:P + T] if kb == 0 else pt[u % 2][:, c, 0:P]
                                    last = pe.matmul(acc, vst[p][:, 2 * b + kb, u, c, :], pr,
                                                     start=(kb == 0 and not odd), stop=(kb == 1 and odd == 1),
                                                     skip_group_check=True)
                            last.then_inc(pv_done.sem, 1)
                        elif kind == "atr":
                            raw_ready.wait(pe, q, s[1] + 1)
                            for j in range(4):
                                last = pe.transpose(ps[:, ONE, j * P:(j + 1) * P], raw[:, j * P:(j + 1) * P],
                                                    ident[:])
                            last.then_inc(at_full.sem, 1)
                        elif kind == "atT":
                            attn_ready.wait(pe, q, 4 * s[1] + 4)
                            for j in range(2):
                                last = pe.transpose(ps[:, ONE, j * P:(j + 1) * P], attn[:, j, :], ident[:])
                            last.then_inc(at_full.sem, 1)
                        elif kind == "wo":
                            attT_ready.wait(pe, q)
                            pe.matmul(ps[:, ONE, :], wo_sb[:], attT[:], start=True, stop=True
                                      ).then_inc(l_full.sem, 1)
                        elif kind == "zt":
                            n = s[1] - 1
                            zT_ready[n].wait(pe, q)
                            for j in range(TT):
                                last = pe.transpose(ps[:, ONE, j * P:(j + 1) * P],
                                                    zT[n][:, j * P:(j + 1) * P], ident[:])
                            last.then_inc((l_full, e_full)[n].sem, 1)
                        elif kind == "x1t":
                            ln_part[0].wait(pe, q)
                            for j in range(TT):
                                last = pe.transpose(ps[:, ONE, j * P:(j + 1) * P], x1[:, j, :], ident[:])
                            last.then_inc(l_full.sem, 1)
                        elif kind == "gu":
                            m = s[1]
                            for name, unit in (("w1", ("g", m)), ("w2", ("u", m))):
                                wait_f_bank(pe, unit, q)
                                ff_group(ps[:, FB[unit[0] == "u"], :], name, [m * P],
                                         lambda k: x1hi[:], lambda k: x1lo[:],
                                         lambda k: x1hi_ready.wait(pe, q),
                                         lambda k: x1lo_ready.wait(pe, q)).then_inc(f_full.sem, 1)
                        elif kind == "h":
                            _, layer, m = s
                            wait_f_bank(pe, s, q)
                            src = (layer + 1) % 2

                            def wait_hi(k):
                                if m == 0 and layer == 1:
                                    h0hi_ready.wait(pe, q, k + 1)
                                elif m == 0:
                                    hhi_ready.wait(pe, q, k + 1)

                            def wait_lo(k):
                                if m == 0:
                                    hlo_ready.wait(pe, q, KT * (layer - 1) + k + 1)

                            ff_group(ps[:, FB[m % 2], :], "h1" if layer == 1 else "h2",
                                     [k * FF + m * P for k in range(KT)],
                                     lambda k: h_hi[src][:, k, :], lambda k: h_lo[src][:, k, :],
                                     wait_hi, wait_lo).then_inc(f_full.sem, 1)
                        elif kind == "w3":
                            ff_group(ps[:, ONE, :], "w3", [k * D for k in range(KT)],
                                     lambda k: h_hi[0][:, k, :], lambda k: h_lo[0][:, k, :],
                                     lambda k: hhi_ready.wait(pe, q, KT + k + 1),
                                     lambda k: hlo_ready.wait(pe, q, 2 * KT + k + 1)
                                     ).then_inc(e_full.sem, 1)

                slots(pe, slot)

            pe.wait_ge(pool_const, POOL_CONSTS)
            pe.wait_ge(lo_summed, 1)
            pe.matmul(ps[0:1, ONE, 0:1], lo_all[:], ones_col[:], start=True, stop=True).then_inc(flag_ready, 1)
            pe.wait_ge(consts_ready, 2)
            flag = pe.value_load(lo_flag[0:1, 0:1].bitcast(I32))
            with pe.If(flag == 0):
                program(split_weights=False)
            with pe.Else():
                program(split_weights=True)

        @block.scalar
        def _(act):
            act.wait_ge(w_in, 16 * W_LOADS)
            nc.scalar.mul(bq_scaled[:], vec_sb[:, 0:1], float(HD) ** -0.5).then_inc(pool_const, 1)
            act.wait_ge(pool_const, POOL_CONSTS)
            act.wait_ge(consts_ready, 1)

            def slot(t, par, stages, before):
                for s, q, p in steps(t, par, stages, ACT_SCHEDULE):
                    kind = s[0]
                    if kind == "qx":
                        q_full.wait(act, q, 1)
                        zT_ready[0].wait(act, q - 2)
                        nc.scalar.copy(xT[p][:], ps[:, ONE, :]).then_inc(xT_ready.sem, 1)
                    elif kind in ("qq", "qk"):
                        w = ("qq", "qk").index(kind)
                        q_full.wait(act, q, 2 + w)
                        qklo_ready.wait(act, q - 1, w + 1)
                        bias = vec_sb[:, 1:2] if w else bq_scaled[:]
                        nc.scalar.activation(qk32[w][:], ps[:, ONE, :], ACT.Identity, bias=bias,
                                             scale=1.0 if w else float(HD) ** -0.5
                                             ).then_inc(qk32_ready.sem, 1)
                    elif kind == "st":
                        _, b, n = s
                        u, c = n // 2, 2 * (n % 2)
                        first, last = SCORE[n % 2]
                        t_full.wait(act, q, HP * b + n + 1)
                        if c == 0:
                            pv_done.wait(act, q, U * b + u - 1)
                        nc.scalar.activation(pt[u % 2][:, c:c + 2, :], ps[:, first:last + 1, 0:3 * P],
                                             ACT.Exp).then_inc(t_free.sem, 1)
                    elif kind == "atr":
                        b = s[1]
                        at_full.wait(act, q, 2 * b + 1)
                        attn_ready.wait(act, q, 4 * b)
                        nc.scalar.copy(rT[:].rearrange("p a k -> p (a k)"), ps[:, ONE, :]
                                       ).then_inc(rT_ready.sem, 1)
                    elif kind == "atT":
                        b = s[1]
                        at_full.wait(act, q, 2 * b + 2)
                        if b == 0:
                            l_full.wait(act, q - 1, 1)
                        nc.scalar.copy(attT[:, b * T:(b + 1) * T], ps[:, ONE, 0:T]
                                       ).then_inc(attT_ready.sem, 1)
                    elif kind == "x1t":
                        l_full.wait(act, q)
                        zT_ready[1].wait(act, q - 1)
                        x1lo_ready.wait(act, q - 1)
                        nc.scalar.copy(x1T[:], ps[:, ONE, :]).then_inc(x1T_ready.sem, 1)
                    elif kind == "gu":
                        m = s[1]
                        unit = ("g", m)
                        f_full.wait(act, q, F_UNITS.index(unit) + 1)
                        f_dve.wait(act, q, m - 1)
                        nc.scalar.activation(sg[:, m % 2, :], ps[:, FB[unit[0] == "u"], :], ACT.Silu,
                                             scale=vec_sb[:, 4 + m:5 + m]).then_inc(f_act.sem, 1)
                    elif kind == "h":
                        _, layer, m = s
                        n = layer * KT + m
                        f_full.wait(act, q, F_UNITS.index(s) + 1)
                        hlo_ready.wait(act, q, n - 3)
                        col = 4 + (1 + layer) * KT + m
                        nc.scalar.activation(hf[:, n % 4, :], ps[:, FB[m % 2], :], ACT.Gelu,
                                             scale=vec_sb[:, col:col + 1]).then_inc(f_act.sem, 1)
                        if (layer, m) == (1, 0):
                            f_full.wait(act, q - 1)
                        f_act.wait(act, q, n + 1)
                        nc.scalar.copy(h_hi[layer % 2][:, m, :], hf[:, n % 4, :]).then_inc(hhi_ready.sem, 1)

            slots(act, slot)

        @block.vector
        def _(dve):
            dve.wait_ge(w_in, 16 * W_LOADS)
            staged = {"w1": hf[:, 0, :], "w2": hf[:, 1, :], "w3": hf[:, 2, :],
                      "h1": vst[0][:].rearrange("p a b c d -> p (a b c d)"),
                      "h2": vst[1][:].rearrange("p a b c d -> p (a b c d)")}
            for n, (name, _) in enumerate(SPLIT):
                if name in ("h1", "h2"):
                    dve.wait_ge(hw_in[name == "h2"], 16)
                nc.vector.tensor_copy(w_hi[name][:], staged[name]).then_inc(split_hi, 1)
                dve.wait_ge(split_hi, n + 1)
                nc.vector.tensor_tensor(w_lo[name][:], staged[name], w_hi[name][:].bitcast(F32),
                                        ALU.subtract).then_inc(split_lo, 1)
                dve.wait_ge(split_lo, n + 1)
                nc.vector.tensor_reduce(lo_max[:, n:n + 1], w_lo[name][:].bitcast(F32), AX_X, ALU.max,
                                        apply_absolute_value=True).then_inc(split_mx, 1)
            dve.wait_ge(split_mx, len(SPLIT))
            nc.vector.tensor_reduce(lo_all[:], lo_max[:], AX_X, ALU.max).then_inc(lo_summed, 1)
            for i in range(2):
                for w, stack in enumerate((qs[i], ks[i])):
                    for u in range(U):
                        nc.vector.tensor_copy(stack[:, u, :], qk32[w][:]).then_inc(split_hi, 1)
                nc.vector.memset(vst[i][:], 0.0).then_inc(split_mx, 1)
            dve.wait_ge(split_mx, len(SPLIT) + 2)
            for i in range(2):
                for odd in range(2):
                    for j in range(TT):
                        nc.vector.memset(vst[i][:, j, odd::2, :, 16 * odd + HD:16 * odd + HD + 1],
                                         1.0).then_inc(split_mx, 1)
            dve.wait_ge(split_mx, len(SPLIT) + 2 + 4 * TT)
            dve.wait_ge(split_hi, len(SPLIT) + 4 * U)
            dve.sem_inc(consts_ready, 1)
            dve.wait_ge(flag_ready, 1)
            nc.vector.tensor_copy(lo_flag[:], ps[0:1, ONE, 0:1]).then_inc(consts_ready, 1)
            dve.wait_ge(pool_const, POOL_CONSTS)
            dve.wait_ge(consts_ready, 2)

            def slot(t, par, stages, before):
                for s, q, p in steps(t, par, stages, DVE_SCHEDULE):
                    kind = s[0]
                    if kind in ("qq", "qk"):
                        w = ("qq", "qk").index(kind)
                        qk32_ready.wait(dve, q, w + 1)
                        stacked.wait(dve, q - 1)
                        nc.vector.tensor_copy(qk_hi[w][:], qk32[w][:]).then_inc(qkhi_ready.sem, 1)
                    elif kind == "qv":
                        q_full.wait(dve, q, 4)
                        pv_done.wait(dve, q - 2)
                        pv = ps[:, ONE, :].rearrange("p (j v e c d) -> p j v e c d", j=TT, v=2, e=2, c=C)
                        bb = bv_sb[:].rearrange("p (j v e c d) -> p j v e c d", j=1, v=2, e=2, c=C)
                        vv = vst[p][:].rearrange("p j (v e) c d -> p j v e c d", e=2)
                        for odd in range(2):
                            nc.vector.tensor_tensor(
                                vv[:, :, :, odd, :, 16 * odd:16 * odd + HD],
                                pv[:, :, :, odd],
                                bb[:, :, :, odd].broadcast_to([P, TT, 2, C, HD]),
                                ALU.add).then_inc(v_ready.sem, 1)
                    elif kind == "s":
                        _, b, n = s
                        u, c = n // 2, 2 * (n % 2)
                        first, last = SCORE[n % 2]
                        s_full.wait(dve, q, HP * b + n + 1)
                        if n == 0:
                            m_step.wait(dve, q, 4 * b)
                        nc.vector.tensor_reduce(
                            mx3[:, c:c + 2, u, :],
                            ps[:, first:last + 1, 0:3 * P].rearrange("p e (a k) -> p e a k", a=3),
                            AX_X, ALU.max).then_inc(s_free.sem, 1)
                    elif kind == "max":
                        b = s[1]
                        s_free.wait(dve, q, HP * (b + 1))
                        nc.vector.tensor_tensor(m32[:, 1], mx3[:, :, :, 0], mx3[:, :, :, 1],
                                                ALU.max).then_inc(m_step.sem, 1)
                        nc.vector.tensor_copy(m32[:, 0], mx3[:, :, :, 2]).then_inc(m_step.sem, 1)
                        m_step.wait(dve, q, 4 * b + 2)
                        mT_full.wait(dve, q, b)
                        nc.vector.tensor_scalar(mhl[:, :, :, 0].bitcast(F32R), m32[:], -1.0, None,
                                                ALU.mult).then_inc(m_step.sem, 1)
                        m_step.wait(dve, q, 4 * b + 3)
                        for it in range(2):
                            last = nc.vector.scalar_tensor_tensor(
                                out=mhl[:, it, :, 1], in0=m32[:, it], scalar=-1.0,
                                in1=mhl[:, it, :, 0], op0=ALU.mult, op1=ALU.subtract)
                        last.then_inc(m_step.sem, 1)
                    elif kind == "mT":
                        b = s[1]
                        mT_full.wait(dve, q, b + 1)
                        m_sent.wait(dve, q, 4 * b)
                        nc.vector.tensor_copy(mT_sb[:], ps[0:32, ONE, 0:T]).then_inc(mT_ready.sem, 1)
                    elif kind == "araw":
                        b = s[1]
                        pv_done.wait(dve, q, 4 * b + 4)
                        at_full.wait(dve, q, 2 * b - 1)
                        nc.vector.tensor_copy(raw[:], ps[:, PVB, :]).then_inc(raw_ready.sem, 1)
                    elif kind == "anorm":
                        b = s[1]
                        rT_ready.wait(dve, q, b + 1)
                        rv = rT[:].rearrange("p a (c e k) -> p a c e k", c=C, e=2)
                        nc.vector.reciprocal(rec[:], rv[:, :, :, :, HD]).then_inc(rec_ready.sem, 1)
                        rec_ready.wait(dve, q, b + 1)
                        at_full.wait(dve, q, 2 * b)
                        for half in range(2):
                            for it in range(2):
                                a = 2 * half + it
                                o = attn[:, it, 64 * half:64 * half + 64].rearrange(
                                    "p (e c d) -> p c e d", e=2, c=C)
                                nc.vector.tensor_tensor(
                                    o, rv[:, a, :, :, 0:HD],
                                    rec[:, a].unsqueeze(3).broadcast_to([P, C, 2, HD]),
                                    ALU.mult).then_inc(attn_ready.sem, 1)
                    elif kind == "wo":
                        l_full.wait(dve, q, 1)
                        l_full.wait(dve, q - 1, 2)
                        nc.vector.scalar_tensor_tensor(
                            out=zT[0][:], in0=ps[:, ONE, :], scalar=vec_sb[:, 2:3],
                            in1=xT[p][:], op0=ALU.add, op1=ALU.add).then_inc(zT_ready[0].sem, 1)
                    elif kind == "lnstat":
                        n = s[1] - 1
                        (l_full, e_full)[n].wait(dve, q, 2)
                        ln_part[n].wait(dve, q - 1)
                        for j in range(TT):
                            nc.vector.bn_stats(st6[n][:, j, :], ps[:, ONE, j * P:(j + 1) * P]
                                               ).then_inc(ln_stats[n].sem, 1)
                        for j in range(TT):
                            if j == 0:
                                ln_stats[n].wait(dve, q)
                                carry(dve, "dve")
                            nc.vector.bn_aggr(mv[n][:, j, :], st6[n][:, j, :]).then_inc(ln_mv[n].sem, 1)
                    elif kind == "lnnorm":
                        n = s[1] - 1
                        ln_rstd[n].wait(dve, q)
                        if n:
                            stored.wait(dve, q - 1)
                        else:
                            l_full.wait(dve, q - 1)
                        dst = o_tok if n else x1
                        for j in range(TT):
                            nc.vector.tensor_scalar(
                                dst[:, j, :], ps[:, ONE, j * P:(j + 1) * P], mv[n][:, j, 0:1],
                                rstd[n][:, j:j + 1], ALU.subtract, ALU.mult).then_inc(ln_part[n].sem, 1)
                    elif kind == "x1t":
                        x1T_ready.wait(dve, q)
                        f_full.wait(dve, q - 1, 2 * KT)
                        nc.vector.tensor_copy(x1hi[:], x1T[:]).then_inc(x1hi_ready.sem, 1)
                    elif kind == "gu":
                        m = s[1]
                        unit = ("u", m)
                        f_full.wait(dve, q, F_UNITS.index(unit) + 1)
                        f_act.wait(dve, q, F_BY_ACT.index(("g", m)) + 1)
                        hlo_ready.wait(dve, q, m - 3)
                        nc.vector.scalar_tensor_tensor(
                            out=hf[:, m % 4, :], in0=ps[:, FB[unit[0] == "u"], :],
                            scalar=vec_sb[:, 4 + KT + m:5 + KT + m], in1=sg[:, m % 2, :],
                            op0=ALU.mult, op1=ALU.mult).then_inc(f_dve.sem, 1)
                        f_dve.wait(dve, q, m + 1)
                        if m == 0:
                            e_full.wait(dve, q - 1, 1)
                        nc.vector.tensor_copy(h_hi[0][:, m, :], hf[:, m % 4, :]).then_inc(h0hi_ready.sem, 1)
                    elif kind == "w3":
                        e_full.wait(dve, q, 1)
                        e_full.wait(dve, q - 1, 2)
                        nc.vector.scalar_tensor_tensor(
                            out=zT[1][:], in0=ps[:, ONE, :], scalar=vec_sb[:, 3:4],
                            in1=x1T[:], op0=ALU.mult, op1=ALU.add).then_inc(zT_ready[1].sem, 1)

            slots(dve, slot)

        @block.gpsimd
        def _(pool):
            nc.gpsimd.memset(ident[:], 0.0).then_inc(pool_const, 1)
            nc.gpsimd.memset(ident_bf[:], 0.0).then_inc(pool_const, 1)
            nc.gpsimd.memset(mask2[:], 0.0).then_inc(pool_const, 1)
            nc.gpsimd.memset(neg_half[:], -0.5).then_inc(pool_const, 1)
            nc.gpsimd.memset(ones_col[:], 1.0).then_inc(pool_const, 1)
            pool.wait_ge(pool_const, 6)
            for m in (ident, ident_bf):
                nc.gpsimd.affine_select(out=m[:], in_=m[:], compare_op=ALU.not_equal, fill=1.0, base=0,
                                        pattern=[[-1, P]], channel_multiplier=1).then_inc(pool_const, 1)
            nc.gpsimd.affine_select(out=mask2[:], in_=mask2[:], compare_op=ALU.is_ge, fill=BIG, base=0,
                                    pattern=[[0, 2], [-1, P]], channel_multiplier=1).then_inc(pool_const, 1)

            def slot(t, par, stages, before):
                for s, q, p in steps(t, par, stages):
                    kind = s[0]
                    if kind in ("qq", "qk"):
                        w = ("qq", "qk").index(kind)
                        qkhi_ready.wait(pool, q, w + 1)
                        stacked.wait(pool, q - 1)
                        nc.gpsimd.tensor_tensor(qk_lo[w][:], qk32[w][:], qk_hi[w][:].bitcast(F32),
                                                ALU.subtract).then_inc(qklo_ready.sem, 1)
                    elif kind == "sel":
                        _, b, u = s
                        t_free.wait(pool, q, HP * b + 2 * u + 2)
                        carry(pool, "pool")
                        diag = pt[u % 2][:, :, 0:2 * P]
                        nc.gpsimd.affine_select(out=diag, in_=diag, compare_op=ALU.is_ge, fill=0.0, base=0,
                                                pattern=[[0, C], [0, 2], [1, P]],
                                                channel_multiplier=-1).then_inc(masked.sem, 1)
                    elif kind == "lnstat":
                        n = s[1] - 1
                        ln_mv[n].wait(pool, q)
                        carry(pool, "pool")
                        nc.gpsimd.tensor_scalar(ve[n][:], mv[n][:, :, 1], EPS, None, ALU.add
                                                ).then_inc(ln_ve[n].sem, 1)
                        ln_ve[n].wait(pool, q)
                        nc.gpsimd.tensor_tensor(rstd[n][:], ve[n][:], neg_half[:], ALU.pow
                                                ).then_inc(ln_rstd[n].sem, 1)
                    elif kind == "x1t":
                        x1hi_ready.wait(pool, q)
                        nc.gpsimd.tensor_tensor(x1lo[:], x1T[:], x1hi[:].bitcast(F32),
                                                ALU.subtract).then_inc(x1lo_ready.sem, 1)
                    elif kind in ("gu", "h"):
                        layer, m = (0, s[1]) if kind == "gu" else (s[1], s[2])
                        n = layer * KT + m
                        if layer:
                            hhi_ready.wait(pool, q, n - KT + 1)
                        else:
                            h0hi_ready.wait(pool, q, m + 1)
                        nc.gpsimd.tensor_tensor(h_lo[layer % 2][:, m, :], hf[:, n % 4, :],
                                                h_hi[layer % 2][:, m, :].bitcast(F32),
                                                ALU.subtract).then_inc(hlo_ready.sem, 1)

            slots(pool, slot)


W_LOADS = 11
POOL_CONSTS = 9


def stack_rows():
    pos = np.tile(np.arange(T), 2).astype(np.float32)
    q = np.zeros((C, 32, TOK), np.float32)
    k = np.zeros((C, 32, TOK), np.float32)
    q[:, 0], k[:, 0] = 1.0, pos
    q[:, 1], k[:, 1] = -pos, 1.0
    for row, edge in ((2, 64), (3, 192)):
        q[:, row], k[:, row] = np.where(pos < edge, BIG, 0.0), (pos >= edge)
    k[:, ROW_MAX:ROW_MAX + 2] = 1.0
    return q.reshape(P, TOK), k.reshape(P, TOK)


def kernel(**inputs):
    import concourse.bacc as _bacc
    from concourse import mybir as _mybir
    from concourse.bass_utils import run_bass_kernel_spmd as _run

    a = {k: np.asarray(v) for k, v in inputs.items()}
    order = np.arange(D).reshape(U, C, HD).transpose(1, 2, 0).reshape(-1)

    def tiles(w):
        o, i = w.shape
        return w.T.reshape(i // P, P, o).transpose(1, 0, 2).reshape(P, -1)

    vecs = np.concatenate(
        [a["L0_attn_bq"][order].reshape(P, 1), a["L0_attn_bk"][order].reshape(P, 1),
         a["L0_attn_bo"].reshape(P, 1), a["L0_ffn_w3_s"].reshape(P, 1)]
        + [a[n].reshape(KT, P).T for n in ("L0_ffn_w1_s", "L0_ffn_w2_s", "L0_ffn_h1_s", "L0_ffn_h2_s")], axis=1)
    qrows, krows = stack_rows()
    arrays = {
        "x": a["L0_attn_x"].reshape(PAIRS, TT, P, D).transpose(0, 2, 1, 3),
        "wq": a["L0_attn_Wq"][order].T, "wk": a["L0_attn_Wk"][order].T,
        "wv": a["L0_attn_Wv"].T, "wo": a["L0_attn_Wo"].T,
        "vecs": vecs, "bv": a["L0_attn_bv"].reshape(1, D),
        "w1": tiles(a["L0_ffn_w1_w"]), "w2": tiles(a["L0_ffn_w2_w"]),
        "h1": tiles(a["L0_ffn_h1_w"]), "h2": tiles(a["L0_ffn_h2_w"]), "w3": tiles(a["L0_ffn_w3_w"]),
        "qrows": qrows, "krows": krows,
    }
    nc = _bacc.Bacc("TRN2", target_bir_lowering=False, num_devices=1)
    feed, args = {}, []
    for name, v in arrays.items():
        feed[f"in_{name}"] = np.ascontiguousarray(v)
        args.append(nc.dram_tensor(f"in_{name}", v.shape, _mybir.dt.from_np(v.dtype), kind="ExternalInput").ap())
    out = nc.dram_tensor("out_0", (PAIRS, P, TT, D), F32, kind="ExternalOutput").ap()
    build_layer(nc, *args, out)
    r = _run(nc, [feed], core_ids=[0])
    got = np.asarray(r.results[0]["out_0"])
    return got.reshape(PAIRS, P, TT, D).transpose(0, 2, 1, 3).reshape(B, T, D)
```

```python
from contextlib import ExitStack

import numpy as np

import concourse.bass as bass
from concourse import mybir

F32 = mybir.dt.float32
F32R = mybir.dt.float32r
BF16 = mybir.dt.bfloat16
I32 = mybir.dt.int32
ALU = mybir.AluOpType
ACT = mybir.ActivationFunctionType
AX_X = mybir.AxisListType.X

P = 128
B, T, D = 32, 256, 128
H, HD = 16, 8
FF = 512
KT = FF // P
PAIRS = B // 2
TOK = 2 * T
TT = TOK // P
U, C = 4, 4
BIG = -(2.0 ** 100)
EPS = 1e-5

ROW_DATA, ROW_MAX, ROWS = 4, 28, 30
Q_PARTS, K_PARTS = "hlh", "hhl"

AFTER_S = {
    0: [("gu", 0), ("pv", 1, 3)], 1: [("gu", 1), ("araw", 1), ("ghi", 0)], 2: [("gu", 2), ("atr", 1), ("anorm", 1), ("ghi", 1)],
    3: [("gu", 3), ("ghi", 2)], 4: [("atT", 1), ("ghi", 3), ("table", "gelu")],
    5: [("wo",), ("h", 1, 0)], 6: [("h", 1, 1), ("qx",)], 7: [("h", 1, 2), ("qq",)],
    8: [("h", 1, 3)], 9: [("mT", 0), ("qhi",), ("qstack",)], 10: [("h", 2, 0), ("zt", 1), ("lnstat", 1), ("rstd", 1)],
    11: [("h", 2, 1)], 12: [("lnnorm", 1), ("h", 2, 2)], 13: [("h", 2, 3)], 14: [("qk",), ("table", "exp")],
}
AFTER_ST = {
    0: [("w3",)], 1: [("mT", 1), ("res2",)], 2: [("khi",), ("kstack",), ("qv",)], 4: [("zt", 2), ("lnstat", 2)], 5: [("rstd", 2)],
    6: [("x1t",)], 7: [("lnnorm", 2)], 8: [("xload",), ("x1split",)], 11: [("araw", 0)], 13: [("atr", 0), ("anorm", 0)],
    15: [("atT", 0), ("table", "silu")],
}
HP = H // 2


def make_schedule():
    steps = []
    for n in range(2 * HP):
        steps.append(("s", n // HP, n % HP))
        if n % HP == HP - 1:
            steps.append(("max", n // HP))
        steps += AFTER_S.get(n, [])
    for n in range(2 * HP):
        steps.append(("st", n // HP, n % HP))
        steps.append(("sel", n // HP, n % HP))
        if n % 2 == 1:
            g = n // 2 - 2
            if g >= 0:
                steps.append(("pv", g // U, g % U))
            if g == 2 * U - 3:
                steps.append(("pv", 1, U - 2))
        steps += AFTER_ST.get(n, [])
    return steps


SCHEDULE = make_schedule()
STAGE_L = [("pv", 1, 3), ("araw", 1), ("atr", 1), ("anorm", 1), ("atT", 1),
           ("wo",), ("zt", 1), ("lnstat", 1), ("rstd", 1), ("lnnorm", 1), ("x1t",), ("x1split",)]
PAIR_OF_STAGE = {"Q": 1, "A": 0, "L": -1, "F": -2, "X": 2, "T": 0}


def stage_of(s):
    if s in STAGE_L:
        return "L"
    if s[0] in ("qx", "qq", "qhi", "qstack", "qk", "khi", "kstack", "qv"):
        return "Q"
    if s[0] in ("gu", "ghi", "h", "w3", "res2", "zt", "lnstat", "rstd", "lnnorm"):
        return "F"
    return {"xload": "X", "table": "T"}.get(s[0], "A")


F_UNITS = [(n, m) for m in range(KT) for n in ("g", "u")] + [
    ("h", i, m) for i in (1, 2) for m in range(KT)] + [("w3",), ("zt", 2)]
F_BY_ACT = [u for u in F_UNITS if u[0] in "gh"]
ONE_KINDS = ("qx", "qq", "qk", "qv", "mT", "atr", "atT", "wo", "zt", "x1t")
TABLES = [s for s in SCHEDULE if s[0] == "table"]
ONE_UNITS = [s for s in SCHEDULE if s[0] in ONE_KINDS and s != ("zt", 2)]


def build_layer(nc, x, wq, wk, wv, wo, vecs, bv, w1, w2, h1, h2, w3, qrows, krows, out):
    ctx = ExitStack()
    with ctx:
        def sb(name, shape, dt=F32):
            return ctx.enter_context(nc.sbuf_tensor(name, shape, dt))

        def sem(name):
            return ctx.enter_context(nc.semaphore(name))

        class Signal:

            def __init__(self, name, per, unit=1):
                self.sem, self.per, self.unit = sem(name), per, unit

            def wait(self, eng, pair, k=None):
                v = (pair * self.per + (self.per if k is None else k)) * self.unit
                if isinstance(v, int) and v <= 0:
                    return
                eng.wait_ge(self.sem, v)

        wq_sb, wk_sb = sb("wq_sb", [P, D]), sb("wk_sb", [P, D])
        wv_sb, wo_sb = sb("wv_sb", [P, D]), sb("wo_sb", [P, D])
        vec_sb = sb("vec_sb", [P, 4 + 4 * KT])
        bq_scaled = sb("bq_scaled", [P, 1])
        bv_sb = sb("bv_sb", [P, D])
        ident = sb("ident", [P, P])
        ident_bf = sb("ident_bf", [P, P], BF16)
        mask2 = sb("mask2", [P, 2, P], BF16)
        neg_half = sb("neg_half", [P, TT])
        ones_col = sb("ones_col", [P, 1])
        SPLIT = (("w1", FF), ("w2", FF), ("h1", KT * FF), ("h2", KT * FF), ("w3", KT * D))
        w_hi = {n: sb(n + "_hi", [P, c], F32R) for n, c in SPLIT}
        w_lo = {n: sb(n + "_lo", [P, c], F32R) for n, c in SPLIT}
        lo_max = sb("lo_max", [P, sum(c for _, c in SPLIT) // FF])
        lo_all = sb("lo_all", [P, 1])
        lo_flag = sb("lo_flag", [1, 1])
        table_in, table_out = sb("table_in", [1, 1]), sb("table_out", [1, 1])

        x_tok = sb("x_tok", [P, TT, D])
        xT = [sb(f"xT{i}", [P, TOK]) for i in range(2)]
        qk32 = [sb("q32", [P, TOK]), sb("k32", [P, TOK])]
        qk_hi = [sb("q_hi", [P, TOK], F32R), sb("k_hi", [P, TOK], F32R)]
        qk_lo = [sb("q_lo", [P, TOK], F32R), sb("k_lo", [P, TOK], F32R)]
        qs = [sb(f"qs{i}", [P, U, TOK], F32R) for i in range(2)]
        ks = [sb(f"ks{i}", [P, U, TOK], F32R) for i in range(2)]
        vst = [sb(f"vst{i}", [P, TT, U, C, 32]) for i in range(2)]

        mx3 = sb("mx3", [P, C, U, 3])
        m32 = sb("m32", [P, 2, C, U])
        mhl = sb("mhl", [P, 2, C, 2, U])
        mT_sb = sb("mT_sb", [32, T], F32R)
        pt = [sb(f"pt{i}", [P, C, 3 * P]) for i in range(U)]
        raw = sb("raw", [P, TOK])
        rT = sb("rT", [P, 4, P])
        rec = sb("rec", [P, 4, C, 2])
        attn = sb("attn", [P, 2, D])
        attT = sb("attT", [P, TOK])

        zT = [sb(f"zT{i}", [P, TOK]) for i in (1, 2)]
        st6 = [sb(f"st6_{i}", [P, TT, 6]) for i in (1, 2)]
        mv = [sb(f"mv{i}", [P, TT, 2]) for i in (1, 2)]
        ve = [sb(f"ve{i}", [P, TT]) for i in (1, 2)]
        rstd = [sb(f"rstd{i}", [P, TT]) for i in (1, 2)]
        x1 = sb("x1", [P, TT, D])
        x1T = [sb(f"x1T{i}", [P, TOK]) for i in range(2)]
        x1hi, x1lo = sb("x1hi", [P, TOK], F32R), sb("x1lo", [P, TOK], F32R)
        sg = sb("sg", [P, 2, TOK])
        hf = sb("hf", [P, 4, TOK])
        h_hi = [sb(f"hhi{i}", [P, KT, TOK], F32R) for i in range(2)]
        h_lo = [sb(f"hlo{i}", [P, KT, TOK], F32R) for i in range(2)]
        o_tok = sb("o_tok", [P, TT, D])

        ps = ctx.enter_context(nc.psum_tensor("ps", [P, 8, TOK], F32))
        SCORE, FB, PVB, ONE = ((0, 1), (2, 3)), (4, 5), 6, 7
        LN_BANK = (ONE, FB[1])

        proj_in = sem("proj_in")
        rows_in = sem("rows_in")
        ffn_in = sem("ffn_in")
        bq_ready = sem("bq_ready")
        pool_const, vst_zero = sem("pool_const"), sem("vst_zero")
        rows_done = sem("rows_done")
        split_hi, split_lo, split_mx = sem("split_hi"), sem("split_lo"), sem("split_mx")
        lo_summed, lo_product, flag_ready = sem("lo_summed"), sem("lo_product"), sem("flag_ready")
        x_loaded = Signal("x_loaded", 1, 16)
        q_full = Signal("q_full", 4)
        xT_ready = Signal("xT_ready", 1)
        qk32_ready = Signal("qk32_ready", 2)
        qkhi_ready = Signal("qkhi_ready", 2)
        qklo_ready = Signal("qklo_ready", 2)
        v_ready = Signal("v_ready", 2)
        stacked = Signal("stacked", 24, 16)
        s_full = Signal("s_full", 2 * HP)
        s_free = Signal("s_free", 2 * HP)
        m_step = Signal("m_step", 8)
        mT_full = Signal("mT_full", 2)
        mT_ready = Signal("mT_ready", 2)
        m_sent = Signal("m_sent", 8, 16)
        t_full = Signal("t_full", 2 * HP)
        t_free = Signal("t_free", 2 * HP)
        masked = Signal("masked", 2 * HP)
        pv_done = Signal("pv_done", 8)
        raw_ready = Signal("raw_ready", 2)
        at_full = Signal("at_full", 4)
        rT_ready = Signal("rT_ready", 2)
        rec_ready = Signal("rec_ready", 2)
        attn_ready = Signal("attn_ready", 8)
        attT_ready = Signal("attT_ready", 2)
        l_full = Signal("l_full", 3)
        e_full = Signal("e_full", 2)
        f_full = Signal("f_full", 4 * KT)
        f_act = Signal("f_act", len(F_BY_ACT))
        f_dve = Signal("f_dve", KT)
        zT_ready = [Signal(f"zT{i}_ready", 1) for i in (1, 2)]
        ln_stats = [Signal(f"ln{i}_stats", TT) for i in (1, 2)]
        ln_mv = [Signal(f"ln{i}_mv", TT) for i in (1, 2)]
        ln_ve = [Signal(f"ln{i}_ve", 1) for i in (1, 2)]
        ln_rstd = [Signal(f"ln{i}_rstd", 1) for i in (1, 2)]
        ln_part = [Signal(f"ln{i}_part", TT) for i in (1, 2)]
        x1T_ready = Signal("x1T_ready", 1)
        x1hi_ready = Signal("x1hi_ready", 1)
        x1lo_ready = Signal("x1lo_ready", 1)
        h0hi_ready = Signal("h0hi_ready", KT)
        hhi_ready = Signal("hhi_ready", 2 * KT)
        hlo_ready = Signal("hlo_ready", 3 * KT)
        stored = Signal("stored", 1, 16)

        table_touched = Signal("table_touched", len(TABLES))
        one_read = {("qx",): (xT_ready, 1), ("qq",): (qk32_ready, 1), ("qk",): (qk32_ready, 2),
                    ("qv",): (v_ready, 2), ("mT", 0): (mT_ready, 1), ("mT", 1): (mT_ready, 2),
                    ("atr", 0): (rT_ready, 1), ("atr", 1): (rT_ready, 2),
                    ("atT", 0): (attT_ready, 1), ("atT", 1): (attT_ready, 2),
                    ("wo",): (zT_ready[0], 1), ("x1t",): (x1T_ready, 1), ("zt", 1): (ln_part[0], TT)}

        def wait_one(eng, s, t, stages, before):
            uses = [(v, t - 1) for v in ONE_UNITS if stage_of(v) in before]
            uses += [(v, t) for v in ONE_UNITS[:ONE_UNITS.index(s)] if stage_of(v) in stages]
            if uses:
                v, of = uses[-1]
                signal, k = one_read[v]
                signal.wait(eng, of + PAIR_OF_STAGE[stage_of(v)], k)

        def wait_score_banks(eng, n, pair):
            if n < 2:
                t_free.wait(eng, pair - 1, n - 2 + 2 * HP + 1)
            elif n < 2 * HP + 2:
                s_free.wait(eng, pair, n - 1)
            else:
                t_free.wait(eng, pair, n - 2 * HP - 1)

        def wait_f_bank(eng, unit, pair):
            n = F_UNITS.index(unit)
            if n < 2:
                pair = pair - 1
            last = F_UNITS[n - 2]
            if last in F_BY_ACT:
                f_act.wait(eng, pair, F_BY_ACT.index(last) + 1)
            elif last == ("w3",):
                zT_ready[1].wait(eng, pair)
            elif last == ("zt", 2):
                ln_part[1].wait(eng, pair)
            else:
                f_dve.wait(eng, pair, last[1] + 1)

        def first_slot(slot):
            slot(-1, 1, "QX", "")

        def later_slots(eng, slot):
            full = "ALQFX"
            slot(0, 0, "AQX", "QX")
            slot(1, 1, "ALQX", "AQX")
            slot(2, 0, full, "ALQX")
            slot(3, 1, full, full)
            with eng.Fori(0, (PAIRS - 6) // 2) as i:
                slot(2 * i + 4, 0, full, full)
                slot(2 * i + 5, 1, full, full)
            slot(PAIRS - 2, 0, "ALQF", full)
            slot(PAIRS - 1, 1, "ALF", "ALQF")
            slot(PAIRS, 0, "LF", "ALF")
            slot(PAIRS + 1, 1, "F", "LF")

        def steps(t, par, stages):
            for s in SCHEDULE:
                stage = stage_of(s)
                if stage in stages or stage == "T":
                    d = PAIR_OF_STAGE[stage]
                    yield s, t + d, (par + d) % 2

        spare = [hf[:, m, :] for m in range(4)] + [b[:] for b in (x1T[0], zT[0], zT[1], attT, raw)] + [
            b[:].rearrange("p j d -> p (j d)") for b in (x1, o_tok)]
        pieces = [(name, slice(c, c + FF)) for name, cols in SPLIT for c in range(0, cols, FF)]
        staged = [(name, cols, buf) for (name, cols), buf in zip(pieces, spare)]
        assert len(pieces) == len(spare)
        steps_passed = {n: sem("passed_" + n) for n in ("sp", "dve", "pool")}

        def carry(eng, name):
            eng.sem_inc(steps_passed[name], 1)

        block = ctx.enter_context(nc.Block())

        @block.sync
        def _(sp):
            def load_x(q):
                sp.dma_start(x_tok[:], x[q]).then_inc(x_loaded.sem, 16)

            load_x(0)
            for dst, src in ((wq_sb, wq), (vec_sb, vecs), (wk_sb, wk), (wv_sb, wv)):
                sp.dma_start(dst[:], src).then_inc(proj_in, 16)
            sp.dma_start(bv_sb[:], bv.broadcast_to([P, D])).then_inc(proj_in, 16)
            for i, src in enumerate((qrows, krows)):
                sp.dma_start(sg[:, i, :], src).then_inc(rows_in, 16)
            sp.dma_start(wo_sb[:], wo).then_inc(ffn_in, 16)
            src = {"w1": w1, "w2": w2, "h1": h1, "h2": h2, "w3": w3}
            for name, cols, buf in staged:
                sp.dma_start(buf, src[name][:, cols]).then_inc(ffn_in, 16)
            sp.wait_ge(rows_done, ROWS_DONE)

            def slot(t, par, stages, before):
                for s, q, p in steps(t, par, stages):
                    kind = s[0]
                    if kind == "xload":
                        q_full.wait(sp, q - 1, 1)
                        carry(sp, "sp")
                        load_x(q)
                    elif kind in ("qstack", "kstack"):
                        w = ("qstack", "kstack").index(kind)
                        stack = (qs, ks)[w][p]
                        t_full.wait(sp, q - 2)
                        carry(sp, "sp")
                        qklo_ready.wait(sp, q, w + 1)
                        carry(sp, "sp")
                        for part, letter in enumerate((Q_PARTS, K_PARTS)[w]):
                            src = (qk_hi if letter == "h" else qk_lo)[w]
                            for c in range(C):
                                r = 32 * c + ROW_DATA + HD * part
                                sp.dma_start(stack[r:r + HD, :, :].bitcast(F32),
                                             src[32 * c:32 * c + 32, :].bitcast(F32)
                                             ).then_inc(stacked.sem, 16)
                    elif kind == "mT":
                        b = s[1]
                        mT_ready.wait(sp, q, b + 1)
                        carry(sp, "sp")
                        for c in range(C):
                            r = 32 * c + ROW_MAX
                            sp.dma_start(qs[p][r:r + 2, :, b * T:(b + 1) * T].bitcast(F32),
                                         mT_sb[8 * c:8 * c + 8, :].bitcast(F32)).then_inc(m_sent.sem, 16)
                    elif kind == "lnnorm" and s[1] == 2:
                        ln_part[1].wait(sp, q)
                        carry(sp, "sp")
                        sp.dma_start(out[q], o_tok[:]).then_inc(stored.sem, 16)

            first_slot(slot)
            later_slots(sp, slot)
            stored.wait(sp, PAIRS - 1)

        @block.tensor
        def _(pe):
            def slot_program(split_weights):
                def ff_group(acc, name, col, hi, lo, wait_hi, wait_lo):
                    n = len(col)
                    for k in range(n):
                        wait_hi(k)
                        pe.matmul(acc, w_hi[name][:, col[k]:col[k] + P], hi(k), start=(k == 0), stop=False)
                        if split_weights:
                            pe.matmul(acc, w_lo[name][:, col[k]:col[k] + P], hi(k),
                                      start=False, stop=False)
                    for k in range(n):
                        wait_lo(k)
                        last = pe.matmul(acc, w_hi[name][:, col[k]:col[k] + P], lo(k),
                                         start=False, stop=(k == n - 1))
                    return last

                def slot(t, par, stages, before):
                    for s, q, p in steps(t, par, stages):
                        kind = s[0]
                        if s in ONE_UNITS:
                            wait_one(pe, s, t, stages, before)
                        if kind == "qx":
                            x_loaded.wait(pe, q)
                            for j in range(TT):
                                last = pe.transpose(ps[:, ONE, j * P:(j + 1) * P], x_tok[:, j, :], ident[:])
                            last.then_inc(q_full.sem, 1)
                        elif kind in ("qq", "qk"):
                            w = ("qq", "qk").index(kind)
                            xT_ready.wait(pe, q)
                            pe.matmul(ps[:, ONE, :], (wq_sb, wk_sb)[w][:], xT[p][:],
                                      start=True, stop=True).then_inc(q_full.sem, 1)
                        elif kind == "qv":
                            for j in range(TT):
                                last = pe.matmul(ps[:, ONE, j * P:(j + 1) * P], xT[p][:, j * P:(j + 1) * P],
                                                 wv_sb[:], start=True, stop=True)
                            last.then_inc(q_full.sem, 1)
                        elif kind == "s":
                            _, b, n = s
                            u, banks = n // 2, SCORE[n % 2]
                            if (b, n) == (0, 0):
                                stacked.wait(pe, q)
                            wait_score_banks(pe, HP * b + n, q)
                            for e, bank in enumerate(banks):
                                c = 2 * (n % 2) + e
                                qr = qs[p][32 * c:32 * c + ROW_MAX, u, b * T:(b + 1) * T]
                                kr = ks[p][32 * c:32 * c + ROW_MAX, u, b * T:(b + 1) * T]
                                pe.matmul(ps[:, bank, 0:T], qr[:, P:T], kr, start=True, stop=False,
                                          skip_group_check=True)
                                pe.matmul(ps[:, bank, T:T + P], qr[:, 0:P], kr[:, 0:P], start=False,
                                          stop=False, skip_group_check=True)
                                last = pe.matmul(ps[:, bank, P:T + P], ident_bf[:],
                                                 mask2[:].rearrange("p a k -> p (a k)"),
                                                 start=False, stop=True, skip_group_check=True)
                            last.then_inc(s_full.sem, 1)
                        elif kind == "mT":
                            b = s[1]
                            m_step.wait(pe, q, 4 * b + 4)
                            for it in range(2):
                                last = pe.transpose(ps[0:32, ONE, it * P:(it + 1) * P],
                                                    mhl[:, it].rearrange("p c a u -> p (c a u)"), ident[:])
                            last.then_inc(mT_full.sem, 1)
                        elif kind == "st":
                            _, b, n = s
                            u, banks = n // 2, SCORE[n % 2]
                            if n == 0:
                                m_sent.wait(pe, q, 4 * b + 4)
                            wait_score_banks(pe, 2 * HP + HP * b + n, q)
                            for e, bank in enumerate(banks):
                                c = 2 * (n % 2) + e
                                qr = qs[p][32 * c:32 * c + ROWS, u, b * T:(b + 1) * T]
                                kr = ks[p][32 * c:32 * c + ROWS, u, b * T:(b + 1) * T]
                                pe.matmul(ps[:, bank, 0:P], kr[:, P:T], qr[:, P:T], start=True, stop=False,
                                          skip_group_check=True)
                                last = pe.matmul(ps[:, bank, P:P + T], kr[:, 0:P], qr, start=False,
                                                 stop=True, skip_group_check=True)
                            last.then_inc(t_full.sem, 1)
                        elif kind == "pv":
                            _, b, u = s
                            half, odd = u // 2, u % 2
                            masked.wait(pe, q, HP * b + 2 * u + 2)
                            if u == 0:
                                if b == 0:
                                    v_ready.wait(pe, q)
                                raw_ready.wait(pe, q, b)
                            o = half * T
                            for kb in (0, 1):
                                for c in range(C):
                                    acc = ps[32 * c:32 * c + 32, PVB, o + P * kb:o + T]
                                    pr = pt[u][:, c, P:P + T] if kb == 0 else pt[u][:, c, 0:P]
                                    last = pe.matmul(acc, vst[p][:, 2 * b + kb, u, c, :], pr,
                                                     start=(kb == 0 and not odd), stop=(kb == 1 and odd == 1),
                                                     skip_group_check=True)
                            last.then_inc(pv_done.sem, 1)
                        elif kind == "atr":
                            raw_ready.wait(pe, q, s[1] + 1)
                            for j in range(4):
                                last = pe.transpose(ps[:, ONE, j * P:(j + 1) * P], raw[:, j * P:(j + 1) * P],
                                                    ident[:])
                            last.then_inc(at_full.sem, 1)
                        elif kind == "atT":
                            attn_ready.wait(pe, q, 4 * s[1] + 4)
                            for j in range(2):
                                last = pe.transpose(ps[:, ONE, j * P:(j + 1) * P], attn[:, j, :], ident[:])
                            last.then_inc(at_full.sem, 1)
                        elif kind == "wo":
                            attT_ready.wait(pe, q)
                            pe.matmul(ps[:, ONE, :], wo_sb[:], attT[:], start=True, stop=True
                                      ).then_inc(l_full.sem, 1)
                        elif kind == "zt":
                            n = s[1] - 1
                            if n:
                                wait_f_bank(pe, s, q)
                            zT_ready[n].wait(pe, q)
                            for j in range(TT):
                                last = pe.transpose(ps[:, LN_BANK[n], j * P:(j + 1) * P],
                                                    zT[n][:, j * P:(j + 1) * P], ident[:])
                            last.then_inc((l_full, e_full)[n].sem, 1)
                        elif kind == "x1t":
                            ln_part[0].wait(pe, q)
                            for j in range(TT):
                                last = pe.transpose(ps[:, ONE, j * P:(j + 1) * P], x1[:, j, :], ident[:])
                            last.then_inc(l_full.sem, 1)
                        elif kind == "gu":
                            m = s[1]
                            for name, unit in (("w1", ("g", m)), ("w2", ("u", m))):
                                wait_f_bank(pe, unit, q)
                                ff_group(ps[:, FB[unit[0] == "u"], :], name, [m * P],
                                         lambda k: x1hi[:], lambda k: x1lo[:],
                                         lambda k: x1hi_ready.wait(pe, q),
                                         lambda k: x1lo_ready.wait(pe, q)).then_inc(f_full.sem, 1)
                        elif kind == "h":
                            _, layer, m = s
                            wait_f_bank(pe, s, q)
                            src = (layer + 1) % 2

                            def wait_hi(k):
                                if m == 0 and layer == 1:
                                    h0hi_ready.wait(pe, q, k + 1)
                                elif m == 0:
                                    hhi_ready.wait(pe, q, k + 1)

                            def wait_lo(k):
                                if m == 0:
                                    hlo_ready.wait(pe, q, KT * (layer - 1) + k + 1)

                            ff_group(ps[:, FB[m % 2], :], "h1" if layer == 1 else "h2",
                                     [k * FF + m * P for k in range(KT)],
                                     lambda k: h_hi[src][:, k, :], lambda k: h_lo[src][:, k, :],
                                     wait_hi, wait_lo).then_inc(f_full.sem, 1)
                        elif kind == "w3":
                            wait_f_bank(pe, s, q)
                            ff_group(ps[:, FB[0], :], "w3", [k * D for k in range(KT)],
                                     lambda k: h_hi[0][:, k, :], lambda k: h_lo[0][:, k, :],
                                     lambda k: hhi_ready.wait(pe, q, KT + k + 1),
                                     lambda k: hlo_ready.wait(pe, q, 2 * KT + k + 1)
                                     ).then_inc(e_full.sem, 1)

                return slot

            pe.wait_ge(pool_const, POOL_CONSTS)
            pe.wait_ge(proj_in, 16 * PROJ_LOADS)
            first_slot(slot_program(split_weights=False))
            pe.wait_ge(lo_summed, 1)
            v_ready.wait(pe, 0)
            pe.matmul(ps[0:1, ONE, 0:1], lo_all[:], ones_col[:], start=True, stop=True).then_inc(lo_product, 1)
            pe.wait_ge(flag_ready, 1)
            flag = pe.value_load(lo_flag[0:1, 0:1].bitcast(I32))
            with pe.If(flag == 0):
                later_slots(pe, slot_program(split_weights=False))
            with pe.Else():
                later_slots(pe, slot_program(split_weights=True))

        @block.scalar
        def _(act):
            act.wait_ge(proj_in, 16 * PROJ_LOADS)
            nc.scalar.mul(bq_scaled[:], vec_sb[:, 0:1], float(HD) ** -0.5).then_inc(bq_ready, 1)
            act.wait_ge(bq_ready, 1)
            act.wait_ge(pool_const, POOL_CONSTS)

            def slot(t, par, stages, before):
                for s, q, p in steps(t, par, stages):
                    kind = s[0]
                    if kind == "qx":
                        q_full.wait(act, q, 1)
                        zT_ready[0].wait(act, q - 2)
                        nc.scalar.copy(xT[p][:], ps[:, ONE, :]).then_inc(xT_ready.sem, 1)
                    elif kind in ("qq", "qk"):
                        w = ("qq", "qk").index(kind)
                        q_full.wait(act, q, 2 + w)
                        qklo_ready.wait(act, q - 1, w + 1)
                        bias = vec_sb[:, 1:2] if w else bq_scaled[:]
                        nc.scalar.activation(qk32[w][:], ps[:, ONE, :], ACT.Identity, bias=bias,
                                             scale=1.0 if w else float(HD) ** -0.5
                                             ).then_inc(qk32_ready.sem, 1)
                    elif kind == "st":
                        _, b, n = s
                        u, c = n // 2, 2 * (n % 2)
                        first, last = SCORE[n % 2]
                        t_full.wait(act, q, HP * b + n + 1)
                        if c == 0:
                            pv_done.wait(act, q, U * (b - 1) + u + 1)
                        nc.scalar.activation(pt[u][:, c:c + 2, :], ps[:, first:last + 1, 0:3 * P],
                                             ACT.Exp).then_inc(t_free.sem, 1)
                    elif s == ("araw", 1):
                        pv_done.wait(act, q)
                        at_full.wait(act, q, 1)
                        nc.scalar.copy(raw[:], ps[:, PVB, :]).then_inc(raw_ready.sem, 1)
                    elif kind == "table":
                        table_touched.wait(act, t + 1, TABLES.index(s))
                        nc.scalar.activation(table_out[:], table_in[:],
                                             {"silu": ACT.Silu, "gelu": ACT.Gelu, "exp": ACT.Exp}[s[1]]
                                             ).then_inc(table_touched.sem, 1)
                    elif kind == "atr":
                        b = s[1]
                        at_full.wait(act, q, 2 * b + 1)
                        attn_ready.wait(act, q, 4 * b)
                        nc.scalar.copy(rT[:].rearrange("p a k -> p (a k)"), ps[:, ONE, :]
                                       ).then_inc(rT_ready.sem, 1)
                    elif kind == "atT":
                        b = s[1]
                        at_full.wait(act, q, 2 * b + 2)
                        if b == 0:
                            l_full.wait(act, q - 1, 1)
                        nc.scalar.copy(attT[:, b * T:(b + 1) * T], ps[:, ONE, 0:T]
                                       ).then_inc(attT_ready.sem, 1)
                    elif kind == "x1t":
                        l_full.wait(act, q)
                        zT_ready[1].wait(act, q - 2)
                        x1lo_ready.wait(act, q - 2)
                        nc.scalar.copy(x1T[p][:], ps[:, ONE, :]).then_inc(x1T_ready.sem, 1)
                    elif kind == "gu":
                        m = s[1]
                        unit = ("g", m)
                        f_full.wait(act, q, F_UNITS.index(unit) + 1)
                        f_dve.wait(act, q, m - 1)
                        nc.scalar.activation(sg[:, m % 2, :], ps[:, FB[unit[0] == "u"], :], ACT.Silu,
                                             scale=vec_sb[:, 4 + m:5 + m]).then_inc(f_act.sem, 1)
                    elif kind == "ghi":
                        m = s[1]
                        f_dve.wait(act, q, m + 1)
                        if m == 0:
                            e_full.wait(act, q - 1, 1)
                        nc.scalar.copy(h_hi[0][:, m, :], hf[:, m % 4, :]).then_inc(h0hi_ready.sem, 1)
                    elif kind == "h":
                        _, layer, m = s
                        n = layer * KT + m
                        f_full.wait(act, q, F_UNITS.index(s) + 1)
                        hlo_ready.wait(act, q, n - 3)
                        col = 4 + (1 + layer) * KT + m
                        nc.scalar.activation(hf[:, n % 4, :], ps[:, FB[m % 2], :], ACT.Gelu,
                                             scale=vec_sb[:, col:col + 1]).then_inc(f_act.sem, 1)
                        if (layer, m) == (1, 0):
                            f_full.wait(act, q - 1)
                        f_act.wait(act, q, n + 1)
                        nc.scalar.copy(h_hi[layer % 2][:, m, :], hf[:, n % 4, :]).then_inc(hhi_ready.sem, 1)

            first_slot(slot)
            act.wait_ge(ffn_in, 16 * (1 + len(staged)))
            for name, cols, buf in staged:
                nc.scalar.copy(w_hi[name][:, cols], buf).then_inc(split_hi, 1)
            later_slots(act, slot)

        @block.vector
        def _(dve):
            dve.wait_ge(rows_in, 32)
            for i in range(2):
                for w, stack in enumerate((qs[i], ks[i])):
                    for u in range(U):
                        nc.vector.tensor_copy(stack[:, u, :], sg[:, w, :]).then_inc(rows_done, 1)
            dve.wait_ge(vst_zero, 2)
            for i in range(2):
                for odd in range(2):
                    for j in range(TT):
                        nc.vector.memset(vst[i][:, j, odd::2, :, 16 * odd + HD:16 * odd + HD + 1],
                                         1.0).then_inc(rows_done, 1)
            dve.wait_ge(rows_done, ROWS_DONE)
            dve.wait_ge(proj_in, 16 * PROJ_LOADS)
            dve.wait_ge(pool_const, POOL_CONSTS)

            def slot(t, par, stages, before):
                for s, q, p in steps(t, par, stages):
                    kind = s[0]
                    if kind in ("qhi", "khi"):
                        w = ("qhi", "khi").index(kind)
                        qk32_ready.wait(dve, q, w + 1)
                        stacked.wait(dve, q - 1)
                        nc.vector.tensor_copy(qk_hi[w][:], qk32[w][:]).then_inc(qkhi_ready.sem, 1)
                        qkhi_ready.wait(dve, q, w + 1)
                        nc.vector.tensor_tensor(qk_lo[w][:], qk32[w][:], qk_hi[w][:].bitcast(F32),
                                                ALU.subtract).then_inc(qklo_ready.sem, 1)
                    elif kind == "qv":
                        q_full.wait(dve, q, 4)
                        pv_done.wait(dve, q - 2)
                        pv = ps[:, ONE, :].rearrange("p (j v e c d) -> p j v e c d", j=TT, v=2, e=2, c=C)
                        bb = bv_sb[:].rearrange("p (j v e c d) -> p j v e c d", j=1, v=2, e=2, c=C)
                        vv = vst[p][:].rearrange("p j (v e) c d -> p j v e c d", e=2)
                        for odd in range(2):
                            nc.vector.tensor_tensor(
                                vv[:, :, :, odd, :, 16 * odd:16 * odd + HD],
                                pv[:, :, :, odd],
                                bb[:, :, :, odd].broadcast_to([P, TT, 2, C, HD]),
                                ALU.add).then_inc(v_ready.sem, 1)
                    elif kind == "s":
                        _, b, n = s
                        u, c = n // 2, 2 * (n % 2)
                        first, last = SCORE[n % 2]
                        s_full.wait(dve, q, HP * b + n + 1)
                        if n == 0:
                            m_step.wait(dve, q, 4 * b)
                        nc.vector.tensor_reduce(
                            mx3[:, c:c + 2, u, :],
                            ps[:, first:last + 1, 0:3 * P].rearrange("p e (a k) -> p e a k", a=3),
                            AX_X, ALU.max).then_inc(s_free.sem, 1)
                    elif kind == "max":
                        b = s[1]
                        s_free.wait(dve, q, HP * (b + 1))
                        nc.vector.tensor_tensor(m32[:, 1], mx3[:, :, :, 0], mx3[:, :, :, 1],
                                                ALU.max).then_inc(m_step.sem, 1)
                        nc.vector.tensor_copy(m32[:, 0], mx3[:, :, :, 2]).then_inc(m_step.sem, 1)
                        m_step.wait(dve, q, 4 * b + 2)
                        mT_full.wait(dve, q, b)
                        nc.vector.tensor_scalar(mhl[:, :, :, 0].bitcast(F32R), m32[:], -1.0, None,
                                                ALU.mult).then_inc(m_step.sem, 1)
                        m_step.wait(dve, q, 4 * b + 3)
                        for it in range(2):
                            last = nc.vector.scalar_tensor_tensor(
                                out=mhl[:, it, :, 1], in0=m32[:, it], scalar=-1.0,
                                in1=mhl[:, it, :, 0], op0=ALU.mult, op1=ALU.subtract)
                        last.then_inc(m_step.sem, 1)
                    elif kind == "mT":
                        b = s[1]
                        mT_full.wait(dve, q, b + 1)
                        m_sent.wait(dve, q, 4 * b)
                        nc.vector.tensor_copy(mT_sb[:], ps[0:32, ONE, 0:T]).then_inc(mT_ready.sem, 1)
                    elif s == ("araw", 0):
                        pv_done.wait(dve, q, 4)
                        at_full.wait(dve, q - 1, 3)
                        nc.vector.tensor_copy(raw[:], ps[:, PVB, :]).then_inc(raw_ready.sem, 1)
                    elif kind == "anorm":
                        b = s[1]
                        rT_ready.wait(dve, q, b + 1)
                        rv = rT[:].rearrange("p a (c e k) -> p a c e k", c=C, e=2)
                        nc.vector.reciprocal(rec[:], rv[:, :, :, :, HD]).then_inc(rec_ready.sem, 1)
                        rec_ready.wait(dve, q, b + 1)
                        at_full.wait(dve, q, 2 * b)
                        for half in range(2):
                            for it in range(2):
                                a = 2 * half + it
                                o = attn[:, it, 64 * half:64 * half + 64].rearrange(
                                    "p (e c d) -> p c e d", e=2, c=C)
                                nc.vector.tensor_tensor(
                                    o, rv[:, a, :, :, 0:HD],
                                    rec[:, a].unsqueeze(3).broadcast_to([P, C, 2, HD]),
                                    ALU.mult).then_inc(attn_ready.sem, 1)
                    elif kind == "wo":
                        l_full.wait(dve, q, 1)
                        l_full.wait(dve, q - 1, 2)
                        nc.vector.scalar_tensor_tensor(
                            out=zT[0][:], in0=ps[:, ONE, :], scalar=vec_sb[:, 2:3],
                            in1=xT[p][:], op0=ALU.add, op1=ALU.add).then_inc(zT_ready[0].sem, 1)
                    elif kind == "lnstat":
                        n = s[1] - 1
                        (l_full, e_full)[n].wait(dve, q, 2)
                        ln_part[n].wait(dve, q - 1)
                        for j in range(TT):
                            nc.vector.bn_stats(st6[n][:, j, :], ps[:, LN_BANK[n], j * P:(j + 1) * P]
                                               ).then_inc(ln_stats[n].sem, 1)
                        for j in range(TT):
                            if j == 0:
                                ln_stats[n].wait(dve, q)
                                carry(dve, "dve")
                            nc.vector.bn_aggr(mv[n][:, j, :], st6[n][:, j, :]).then_inc(ln_mv[n].sem, 1)
                    elif kind == "lnnorm":
                        n = s[1] - 1
                        ln_rstd[n].wait(dve, q)
                        if n:
                            stored.wait(dve, q - 1)
                        else:
                            l_full.wait(dve, q - 1)
                        dst = o_tok if n else x1
                        for j in range(TT):
                            nc.vector.tensor_scalar(
                                dst[:, j, :], ps[:, LN_BANK[n], j * P:(j + 1) * P], mv[n][:, j, 0:1],
                                rstd[n][:, j:j + 1], ALU.subtract, ALU.mult).then_inc(ln_part[n].sem, 1)
                    elif kind == "x1split":
                        x1T_ready.wait(dve, q)
                        f_full.wait(dve, q - 1, 2 * KT)
                        nc.vector.tensor_copy(x1hi[:], x1T[p][:]).then_inc(x1hi_ready.sem, 1)
                        x1hi_ready.wait(dve, q)
                        nc.vector.tensor_tensor(x1lo[:], x1T[p][:], x1hi[:].bitcast(F32),
                                                ALU.subtract).then_inc(x1lo_ready.sem, 1)
                    elif kind == "gu":
                        m = s[1]
                        unit = ("u", m)
                        f_full.wait(dve, q, F_UNITS.index(unit) + 1)
                        f_act.wait(dve, q, F_BY_ACT.index(("g", m)) + 1)
                        hlo_ready.wait(dve, q, m - 3)
                        nc.vector.scalar_tensor_tensor(
                            out=hf[:, m % 4, :], in0=ps[:, FB[unit[0] == "u"], :],
                            scalar=vec_sb[:, 4 + KT + m:5 + KT + m], in1=sg[:, m % 2, :],
                            op0=ALU.mult, op1=ALU.mult).then_inc(f_dve.sem, 1)
                    elif kind == "res2":
                        e_full.wait(dve, q, 1)
                        e_full.wait(dve, q - 1, 2)
                        nc.vector.scalar_tensor_tensor(
                            out=zT[1][:], in0=ps[:, FB[0], :], scalar=vec_sb[:, 3:4],
                            in1=x1T[p][:], op0=ALU.mult, op1=ALU.add).then_inc(zT_ready[1].sem, 1)

            first_slot(slot)
            dve.wait_ge(ffn_in, 16 * (1 + len(staged)))
            for n, (name, cols, buf) in enumerate(staged):
                dve.wait_ge(split_hi, n + 1)
                nc.vector.tensor_tensor(w_lo[name][:, cols], buf, w_hi[name][:, cols].bitcast(F32),
                                        ALU.subtract).then_inc(split_lo, 1)
                dve.wait_ge(split_lo, n + 1)
                nc.vector.tensor_reduce(lo_max[:, n:n + 1], w_lo[name][:, cols].bitcast(F32), AX_X, ALU.max,
                                        apply_absolute_value=True).then_inc(split_mx, 1)
            dve.wait_ge(split_mx, len(staged))
            nc.vector.tensor_reduce(lo_all[:], lo_max[:], AX_X, ALU.max).then_inc(lo_summed, 1)
            dve.wait_ge(lo_product, 1)
            nc.vector.tensor_copy(lo_flag[:], ps[0:1, ONE, 0:1]).then_inc(flag_ready, 1)
            later_slots(dve, slot)

        @block.gpsimd
        def _(pool):
            nc.gpsimd.memset(ident[:], 0.0).then_inc(pool_const, 1)
            nc.gpsimd.memset(ident_bf[:], 0.0).then_inc(pool_const, 1)
            nc.gpsimd.memset(mask2[:], 0.0).then_inc(pool_const, 1)
            nc.gpsimd.memset(neg_half[:], -0.5).then_inc(pool_const, 1)
            nc.gpsimd.memset(ones_col[:], 1.0).then_inc(pool_const, 1)
            nc.gpsimd.memset(table_in[:], 0.0).then_inc(pool_const, 1)
            pool.wait_ge(pool_const, 6)
            for m in (ident, ident_bf):
                nc.gpsimd.affine_select(out=m[:], in_=m[:], compare_op=ALU.not_equal, fill=1.0, base=0,
                                        pattern=[[-1, P]], channel_multiplier=1).then_inc(pool_const, 1)
            nc.gpsimd.affine_select(out=mask2[:], in_=mask2[:], compare_op=ALU.is_ge, fill=BIG, base=0,
                                    pattern=[[0, 2], [-1, P]], channel_multiplier=1).then_inc(pool_const, 1)
            for i in range(2):
                nc.gpsimd.memset(vst[i][:], 0.0).then_inc(vst_zero, 1)

            def slot(t, par, stages, before):
                for s, q, p in steps(t, par, stages):
                    kind = s[0]
                    if kind == "sel":
                        _, b, n = s
                        u, c = n // 2, 2 * (n % 2)
                        t_free.wait(pool, q, HP * b + n + 1)
                        carry(pool, "pool")
                        diag = pt[u][:, c:c + 2, 0:2 * P]
                        nc.gpsimd.affine_select(out=diag, in_=diag, compare_op=ALU.is_ge, fill=0.0, base=0,
                                                pattern=[[0, 2], [0, 2], [1, P]],
                                                channel_multiplier=-1).then_inc(masked.sem, 1)
                    elif kind == "rstd":
                        n = s[1] - 1
                        ln_mv[n].wait(pool, q)
                        carry(pool, "pool")
                        nc.gpsimd.tensor_scalar(ve[n][:], mv[n][:, :, 1], EPS, None, ALU.add
                                                ).then_inc(ln_ve[n].sem, 1)
                        ln_ve[n].wait(pool, q)
                        nc.gpsimd.tensor_tensor(rstd[n][:], ve[n][:], neg_half[:], ALU.pow
                                                ).then_inc(ln_rstd[n].sem, 1)
                    elif kind in ("gu", "h"):
                        layer, m = (0, s[1]) if kind == "gu" else (s[1], s[2])
                        n = layer * KT + m
                        if layer:
                            hhi_ready.wait(pool, q, n - KT + 1)
                        else:
                            h0hi_ready.wait(pool, q, m + 1)
                        nc.gpsimd.tensor_tensor(h_lo[layer % 2][:, m, :], hf[:, n % 4, :],
                                                h_hi[layer % 2][:, m, :].bitcast(F32),
                                                ALU.subtract).then_inc(hlo_ready.sem, 1)

            first_slot(slot)
            later_slots(pool, slot)


PROJ_LOADS = 5
POOL_CONSTS = 9
ROWS_DONE = 4 * U + 4 * TT


def stack_rows():
    pos = np.tile(np.arange(T), 2).astype(np.float32)
    q = np.zeros((C, 32, TOK), np.float32)
    k = np.zeros((C, 32, TOK), np.float32)
    q[:, 0], k[:, 0] = 1.0, pos
    q[:, 1], k[:, 1] = -pos, 1.0
    for row, edge in ((2, 64), (3, 192)):
        q[:, row], k[:, row] = np.where(pos < edge, BIG, 0.0), (pos >= edge)
    k[:, ROW_MAX:ROW_MAX + 2] = 1.0
    return q.reshape(P, TOK), k.reshape(P, TOK)


def kernel(**inputs):
    import concourse.bacc as _bacc
    from concourse import mybir as _mybir
    from concourse.bass_utils import run_bass_kernel_spmd as _run

    a = {k: np.asarray(v) for k, v in inputs.items()}
    order = np.arange(D).reshape(U, C, HD).transpose(1, 2, 0).reshape(-1)

    def tiles(w):
        o, i = w.shape
        return w.T.reshape(i // P, P, o).transpose(1, 0, 2).reshape(P, -1)

    vecs = np.concatenate(
        [a["L0_attn_bq"][order].reshape(P, 1), a["L0_attn_bk"][order].reshape(P, 1),
         a["L0_attn_bo"].reshape(P, 1), a["L0_ffn_w3_s"].reshape(P, 1)]
        + [a[n].reshape(KT, P).T for n in ("L0_ffn_w1_s", "L0_ffn_w2_s", "L0_ffn_h1_s", "L0_ffn_h2_s")], axis=1)
    qrows, krows = stack_rows()
    arrays = {
        "x": a["L0_attn_x"].reshape(PAIRS, TT, P, D).transpose(0, 2, 1, 3),
        "wq": a["L0_attn_Wq"][order].T, "wk": a["L0_attn_Wk"][order].T,
        "wv": a["L0_attn_Wv"].T, "wo": a["L0_attn_Wo"].T,
        "vecs": vecs, "bv": a["L0_attn_bv"].reshape(1, D),
        "w1": tiles(a["L0_ffn_w1_w"]), "w2": tiles(a["L0_ffn_w2_w"]),
        "h1": tiles(a["L0_ffn_h1_w"]), "h2": tiles(a["L0_ffn_h2_w"]), "w3": tiles(a["L0_ffn_w3_w"]),
        "qrows": qrows, "krows": krows,
    }
    nc = _bacc.Bacc("TRN2", target_bir_lowering=False, num_devices=1)
    feed, args = {}, []
    for name, v in arrays.items():
        feed[f"in_{name}"] = np.ascontiguousarray(v)
        args.append(nc.dram_tensor(f"in_{name}", v.shape, _mybir.dt.from_np(v.dtype), kind="ExternalInput").ap())
    out = nc.dram_tensor("out_0", (PAIRS, P, TT, D), F32, kind="ExternalOutput").ap()
    build_layer(nc, *args, out)
    r = _run(nc, [feed], core_ids=[0])
    got = np.asarray(r.results[0]["out_0"])
    return got.reshape(PAIRS, P, TT, D).transpose(0, 2, 1, 3).reshape(B, T, D)
```
